# Optimizing a Trainium2 kernel written in Bass

```python
import numpy as np
import jax
import jax.numpy as jnp

def _softmax(x, axis=-1):
    return jax.nn.softmax(x, axis=axis)

def _gelu(x):
    return jax.nn.gelu(x, approximate=True)

def _silu(x):
    return jax.nn.silu(x)

def _sigmoid(x):
    return jax.nn.sigmoid(x)

def _layernorm(x, axis=-1, eps=1e-05):
    m = jnp.mean(x, axis=axis, keepdims=True)
    v = jnp.var(x, axis=axis, keepdims=True)
    return (x - m) / jnp.sqrt(v + eps)

def _scatter_add(tgt, idx, src, axis=0):
    return tgt.at[idx].add(src)

def _segment_sum(src, seg, n):
    return jax.ops.segment_sum(src, seg, n)
kernel_name = 'mk_adj_preln_d2_adj_r2_7ed9c2'

def setup_inputs(seed: int=0):
    np.random.seed(seed)
    _w = jnp.asarray

    def _rec_inputs():
        import jax
        import jax.numpy as jnp
        _gk = jax.random.key(seed)
        x = 7.22e-05 + 1 * jax.random.normal(jax.random.fold_in(_gk, 1), (4096, 256), jnp.float32)
        _a = jax.random.bernoulli(jax.random.fold_in(_gk, 2), 0.000488281, (4096, 4096))
        _a = jnp.logical_or(_a, jnp.eye(4096, dtype=bool))
        _af = _a.astype(jnp.float32)
        _af = _af * jax.random.uniform(jax.random.fold_in(_gk, 3), (4096, 4096), jnp.float32, 0.05, 1)
        adj = _af
        return (x, adj)
    x, adj = _rec_inputs()

    def _L0_gnn_setup():
        import jax, jax.numpy as jnp
        import numpy as np
        N, NFEAT, NHID = (8192, 256, 256)

        def _gc_layer(x, adj, W):
            support = adj @ x
            h = jnp.concatenate([x, support], axis=1)
            return h @ W
        key = jax.random.key(seed)
        k1, k2, k3, k4 = jax.random.split(key, 4)
        x = jax.random.normal(k1, (N, NFEAT), dtype=jnp.float32)
        adj = jax.random.uniform(k2, (N, N), dtype=jnp.float32)
        stdv1 = 1.0 / np.sqrt(NHID)
        W1 = jax.random.uniform(k3, (2 * NFEAT, NHID), dtype=jnp.float32, minval=-stdv1, maxval=stdv1)
        W2 = jax.random.uniform(k4, (2 * NHID, NHID), dtype=jnp.float32, minval=-stdv1, maxval=stdv1)
        return {'x': x, 'adj': adj, 'W1': W1, 'W2': W2}
    _L0_gnn_all = _L0_gnn_setup()
    _L0_gnn_in = {k: v for k, v in _L0_gnn_all.items() if k in ('W1', 'W2')}
    del _L0_gnn_all

    def _L1_gnn_setup():
        import jax, jax.numpy as jnp
        import numpy as np
        N = 4096
        D = 256
        EPS = 1e-12
        key = jax.random.key(seed)
        k1, k2 = jax.random.split(key)
        cur = jax.random.normal(k1, (N, D), dtype=jnp.float32)
        incidence_m = jax.random.normal(k2, (N, N), dtype=jnp.float32)
        return {'cur': cur, 'incidence_m': incidence_m}
    _L1_gnn_all = _L1_gnn_setup()
    _L1_gnn_in = {k: v for k, v in _L1_gnn_all.items() if k in ()}
    del _L1_gnn_all
    return {'x': x, 'adj': adj, 'L0_gnn_W1': _L0_gnn_in['W1'], 'L0_gnn_W2': _L0_gnn_in['W2']}

def reference(x, adj, L0_gnn_W1, L0_gnn_W2):
    import jax
    import jax.numpy as jnp

    def _L0_gnn_ref(x, adj, W1, W2):
        import jax, jax.numpy as jnp
        import numpy as np
        N, NFEAT, NHID = (8192, 256, 256)

        def _gc_layer(x, adj, W):
            support = adj @ x
            h = jnp.concatenate([x, support], axis=1)
            return h @ W
        h = jax.nn.relu(_gc_layer(x, adj, W1))
        h = jax.nn.relu(_gc_layer(h, adj, W2))
        return h

    def _L1_gnn_ref(cur, incidence_m):
        import jax, jax.numpy as jnp
        import numpy as np
        N = 4096
        D = 256
        EPS = 1e-12
        mask = incidence_m > 0
        head = jax.lax.stop_gradient(mask.astype(incidence_m.dtype))
        head = head / jnp.maximum(jnp.sqrt(jnp.sum(head * head, axis=-1, keepdims=True)), EPS)
        inc = incidence_m + head
        edge_fea = inc @ cur
        edge_degree = jnp.sum(inc, axis=-1, keepdims=True)
        return edge_fea / edge_degree
    h = jnp.maximum(_layernorm(x, axis=-1), 0.0)
    x = x + _L0_gnn_ref(h, adj, L0_gnn_W1, L0_gnn_W2)
    h = jnp.maximum(_layernorm(x, axis=-1), 0.0)
    x = x + _L1_gnn_ref(h, adj)
    return x

_drawn_inputs = setup_inputs


def setup_inputs(seed=0):
    import zlib

    import numpy as np

    out = dict(_drawn_inputs(seed))
    spreads = {}
    factors = {}
    for name, (base, spread) in spreads.items():
        noise = np.random.default_rng([zlib.crc32(name.encode()), seed]).standard_normal(out[name].shape)
        drawn = base * np.exp(spread * noise) if base else spread * noise
        out[name] = jnp.asarray(drawn.astype(out[name].dtype))
    for name, factor in factors.items():
        out[name] = (out[name] * factor).astype(out[name].dtype)
    return out
```

```python
import concourse.bass as bass
from concourse import mybir
from contextlib import ExitStack

P = 128
N = 4096
D = 256
K = D // P
BW = 512
NB = N // BW
IT = BW // P
CT = 2
CW = CT * BW
NC = N // (P * CT)
RING = 4
SPLIT = 2
LN_EPS = 1e-5
NORM_EPS = 1e-12
GRAPH_1, GRAPH_2, HYPER = range(3)
WA_1, WB, WA_2 = range(3)
HI, LO = range(2)

TAKE = 1
MAKE = 4
SPLIT_MADE = 6
STATS, NORM, SPLIT_NORM = 6, 8, 9
COUNT, COUNT_TAKE = 11, 13
FINISH = 9
LN_STEPS = 6


def gnn_kernel(nc, adj_t, x_rows, x_cols, w, out, h_mem, x1_mem, rn_mem, rd_mem):
    f32, f32r = mybir.dt.float32, mybir.dt.float32r
    ALU, ACT = mybir.AluOpType, mybir.ActivationFunctionType

    with ExitStack() as ctx:
        def sb(name, shape, dt=f32, where=ctx):
            return where.enter_context(nc.sbuf_tensor(name, shape, dt))

        def sem(name):
            return ctx.enter_context(nc.semaphore(name))

        g_hi = [sb(f"g_hi{s}", [P, N // P, D], f32r) for s in range(2)]
        g_lo = [sb(f"g_lo{s}", [P, N // P, D], f32r) for s in range(2)]
        raw = sb("raw", [P, RING, CW])
        hi = sb("hi", [P, SPLIT, CW], f32r)
        lo = sb("lo", [P, SPLIT, CW], f32r)
        w_hi = sb("w_hi", [P, 3, K, D], f32r)
        w_lo = sb("w_lo", [P, 3, K, D], f32r)
        h_old = sb("h_old", [P, 2, K, BW], f32r)
        xblk = sb("xblk", [P, K, BW])
        nat = sb("nat", [P, IT, D])
        acc = sb("acc", [P, CW])
        acc_end = sb("acc_end", [P, CW])
        ident = sb("ident", [P, P])
        ones = sb("ones", [P, 1])
        stats = sb("stats", [P, IT, 6])
        mv = sb("mv", [P, IT, 2])
        var = sb("var", [P, IT])
        root = sb("root", [P, IT])
        quot = sb("quot", [P, IT])
        rstd = sb("rstd", [P, IT])
        nmean = sb("nmean", [P, IT])
        cnt = sb("cnt", [P, N // P])
        rsum = sb("rsum", [P, N // P])
        col_a = sb("col_a", [P, N // P])
        col_b = sb("col_b", [P, N // P])
        rn = sb("rn", [P, N // P])
        rdeg = sb("rdeg", [P, N // P])
        row = sb("row", [N // P, P])
        with ExitStack() as early:
            h_new = sb("h_new", [P, 2, K, BW], f32r, early)
        rn_row = sb("rn_row", [P, 2, BW])
        rd_row = sb("rd_row", [P, BW])

        main = ctx.enter_context(nc.psum_tensor("main", [P, 2, K, BW], f32))
        turned = ctx.enter_context(nc.psum_tensor("turned", [P, K, BW], f32))
        made = ctx.enter_context(nc.psum_tensor("made", [P, IT, D], f32))

        rows_in = [nat[:, :, :], acc[:, :].rearrange("p (t d) -> p t d", t=IT)]
        acc_t = acc[:, :].rearrange("p (t n) -> p t n", t=CT)

        raw_full = [sem(f"raw_full{r}") for r in range(RING)]
        inc_ready = sem("inc_ready")
        hi_ready = sem("hi_ready")
        lo_ready = sem("lo_ready")
        acc_step = sem("acc_step")
        chunk_done = sem("chunk_done")
        h_hi_ready = sem("h_hi_ready")
        h_lo_ready = sem("h_lo_ready")
        h_stored = sem("h_stored")
        h_loaded = sem("h_loaded")
        h_used = sem("h_used")
        turned_done = sem("turned_done")
        made_done = sem("made_done")
        g_hi_ready = sem("g_hi_ready")
        g_lo_ready = sem("g_lo_ready")
        x_loaded = [sem(f"x_loaded{s}") for s in range(2)]
        rows_ready = sem("rows_ready")
        xblk_loaded = sem("xblk_loaded")
        xblk_ready = sem("xblk_ready")
        xblk_stored = sem("xblk_stored")
        out_stored = sem("out_stored")
        ln_step = sem("ln_step")
        var_ready = sem("var_ready")
        root_ready = sem("root_ready")
        rstd_ready = sem("rstd_ready")
        centred = sem("centred")
        scaled = sem("scaled")
        w_loaded = sem("w_loaded")
        w_hi_ready = sem("w_hi_ready")
        w_lo_ready = sem("w_lo_ready")
        cols_done = sem("cols_done")
        cols_taken = sem("cols_taken")
        cols_step = sem("cols_step")
        norm_root = sem("norm_root")
        row_turned = sem("row_turned")
        row_ready = sem("row_ready")
        row_stored = sem("row_stored")
        rn_loaded = [sem(f"rn_loaded{s}") for s in range(2)]
        rd_loaded = sem("rd_loaded")
        product = sem("product")
        const_step = sem("const_step")
        stats_seen = sem("stats_seen")
        block_seen = sem("block_seen")

        block = ctx.enter_context(nc.Block())

        def blocks(eng, one):
            for layer in (GRAPH_1, GRAPH_2, HYPER):
                for b in range(2):
                    one(NB * layer + b, layer, b, b)
                with eng.Fori(1, NB // 2) as pair:
                    for half in range(2):
                        b = 2 * pair + half
                        one(b + NB * layer, layer, b, half)

        def pairs(eng, one):
            one(0, 0)
            one(1, 1)
            with eng.Fori(1, NB // 2) as pair:
                for half in range(2):
                    one(2 * pair + half, half)

        def is_first(q):
            return isinstance(q, int) and q == 0

        def is_at(q, number):
            return isinstance(q, int) and q == number

        def before(q, layer, b):
            if isinstance(b, int) and b == 0:
                return layer - 1, NB - 1
            return layer, b - 1

        def tiles(b):
            return bass.ds(b * IT, IT)

        W_ORDER = [(1, WB), (0, WA_1), (2, WA_2), (3, WB)]

        @block.sync
        def _(sp):
            def one(q, layer, b, half):
                for c in range(NC):
                    if not (is_first(q) and c < RING):
                        sp.wait_ge(hi_ready, q * NC + (c - RING + 1))
                        sp.wait_ge(lo_ready, q * NC + (c - RING + 1))
                    sp.dma_start(raw[:, c % RING, :], adj_t[b, c, :, :]).then_inc(raw_full[c % RING], 16)

            blocks(sp, one)

        @block.gpsimd
        def _(pool):
            pool.dma_start(rows_in[0], x_rows[0, :, :, :]).then_inc(x_loaded[0], 16)
            pool.dma_start(rows_in[1], x_rows[1, :, :, :]).then_inc(x_loaded[1], 16)
            nc.gpsimd.memset(ident[:, :], 0.0).then_inc(const_step, 1)
            nc.gpsimd.memset(ones[:, :], 1.0).then_inc(const_step, 1)
            pool.wait_ge(const_step, 2)
            nc.gpsimd.affine_select(out=ident[:, :], in_=ident[:, :], compare_op=ALU.not_equal, fill=1.0,
                                    base=0, pattern=[[-1, P]], channel_multiplier=1).then_inc(const_step, 1)

            def load_w(n):
                if n:
                    pool.wait_ge(w_hi_ready, n)
                    pool.wait_ge(w_lo_ready, n)
                pool.dma_start(xblk[:, 0, :], w[W_ORDER[n][0], :, :]).then_inc(w_loaded, 16)

            def load_x(b, half):
                pool.wait_ge(turned_done, b - 1)
                pool.dma_start(rows_in[half], x_rows[b, :, :, :]).then_inc(x_loaded[half], 16)

            def store_h(number, layer, b):
                pool.wait_ge(h_hi_ready, number)
                pool.wait_ge(h_lo_ready, number)
                pool.dma_start(h_mem[layer, b, :, :], h_new[:, :, :, :].rearrange("p s k n -> p (s k n)")
                               ).then_inc(h_stored, 16)
                pool.wait_ge(h_stored, number * 16)

            def load_h(q, layer, b):
                if not is_first(q):
                    pool.wait_ge(h_used, q)
                pool.dma_start(h_old[:, :, :, :].rearrange("p s k n -> p (s k n)"), h_mem[layer, b, :, :]
                               ).then_inc(h_loaded, 16)

            for n in range(3):
                load_w(n)
            store_h(1, GRAPH_1, 0)
            load_h(0, GRAPH_1, 0)
            with pool.Fori(1, NB // 2) as pair:
                load_x(2 * pair, 0)
                store_h(2 * pair, GRAPH_1, 2 * pair - 1)
                load_x(2 * pair + 1, 1)
                store_h(2 * pair + 1, GRAPH_1, 2 * pair)
            store_h(NB, GRAPH_1, NB - 1)
            load_w(3)

            with pool.Fori(0, NB - 1) as b:
                load_h(b + 1, GRAPH_1, b + 1)
                store_h(b + (NB + 1), GRAPH_2, b)
            load_h(NB, GRAPH_2, 0)
            store_h(2 * NB, GRAPH_2, NB - 1)
            pool.wait_ge(w_hi_ready, 4)
            pool.wait_ge(w_lo_ready, 4)

            def load_xblk(source):
                pool.dma_start(xblk[:, :, :].rearrange("p k n -> p (k n)"), source).then_inc(xblk_loaded, 16)

            def load_x_cols(b):
                if not is_at(b, 0):
                    pool.wait_ge(made_done, b + 2 * NB)
                load_xblk(x_cols[b, :, :])

            def store_x1(b):
                pool.wait_ge(xblk_ready, b + 1)
                pool.sem_inc(block_seen, 1)
                pool.dma_start(x1_mem[b, :, :], xblk[:, :, :].rearrange("p k n -> p (k n)")
                               ).then_inc(xblk_stored, 16)
                pool.wait_ge(xblk_stored, (b + 1) * 16)

            def spread(dest, mem, b, done):
                pool.dma_start(dest, mem[bass.ds(b, 1), :].partition_broadcast(P)).then_inc(done, 16)

            def store_row(number, mem):
                pool.wait_ge(row_ready, number)
                pool.dma_start(mem.rearrange("b (t p) -> (b t) p", p=P), row[:, :]).then_inc(row_stored, 16)
                pool.wait_ge(row_stored, number * 16)

            load_x_cols(0)
            load_h(NB + 1, GRAPH_2, 1)
            store_x1(0)
            store_row(1, rn_mem)
            for half in range(2):
                spread(rn_row[:, half, :], rn_mem, half, rn_loaded[half])
            with pool.Fori(1, NB - 1) as b:
                load_x_cols(b)
                load_h(b + (NB + 1), GRAPH_2, b + 1)
                store_x1(b)
            load_x_cols(NB - 1)
            store_x1(NB - 1)
            store_row(2, rd_mem)

            pool.wait_ge(made_done, 3 * NB)

            def last(b, half, more):
                load_xblk(x1_mem[b, :, :])
                spread(rd_row[:, :], rd_mem, b, rd_loaded)
                if more:
                    pool.wait_ge(lo_ready, b * NC + (2 * NB + 1) * NC)
                    spread(rn_row[:, half, :], rn_mem, b + 2, rn_loaded[half])
                pool.wait_ge(xblk_ready, b + (NB + 1))
                pool.sem_inc(block_seen, 1)
                pool.dma_start(out[b, :, :], xblk[:, :, :].rearrange("p k n -> p (k n)")
                               ).then_inc(out_stored, 16)
                pool.wait_ge(out_stored, b * 16 + 16)

            with pool.Fori(0, NB // 2 - 1) as pair:
                for half in range(2):
                    last(2 * pair + half, half, True)
            for half in range(2):
                last(NB - 2 + half, half, False)

        @block.scalar
        def _(act):
            def split_w(n):
                act.wait_ge(w_loaded, 16 * (n + 1))
                if n == 3:
                    act.wait_ge(made_done, NB)
                nc.scalar.activation(w_hi[:, W_ORDER[n][1], :, :],
                                     xblk[:, 0, :].rearrange("p (k d) -> p k d", k=K),
                                     ACT.Copy).then_inc(w_hi_ready, 1)

            def ln_root(n):
                act.wait_ge(var_ready, n)
                nc.scalar.activation(root[:, :], var[:, :], ACT.Sqrt).then_inc(root_ready, 1)

            def h_from(source, number):
                if not is_at(number, 1):
                    act.wait_ge(h_stored, (number - 1) * 16)
                    act.wait_ge(made_done, number - 1)
                nc.scalar.activation(h_new[:, HI, :, :], source, ACT.Relu).then_inc(h_hi_ready, 1)

            def g_from(source, dest, b, number):
                nc.scalar.activation(dest[:, tiles(b), :], source, ACT.Copy).then_inc(g_hi_ready, 1)

            def head(b, half):
                if not is_at(b, 0):
                    act.wait_ge(turned_done, b)
                    h_from(turned[:, :, :], b)
                ln_root(b + 1)
                if not is_at(b, 0):
                    act.wait_ge(made_done, b)
                    g_from(made[:, :, :], g_hi[0], b - 1, b)

            for n in range(3):
                split_w(n)
            pairs(act, head)
            act.wait_ge(turned_done, NB)
            h_from(turned[:, :, :], NB)
            act.wait_ge(made_done, NB)
            g_from(made[:, :, :], g_hi[0], NB - 1, NB)
            split_w(3)

            def after_graph_1(c, q, b, half):
                if c == TAKE:
                    act.wait_ge(chunk_done, q * NC)
                    h_from(main[:, half, :, :], q + NB)
                if c == SPLIT_MADE:
                    act.wait_ge(made_done, q + NB)
                    g_from(made[:, :, :], g_hi[1], b, q + NB)

            def after_graph_2(c, q, b, half):
                if c == STATS:
                    ln_root(q)
                if c == NORM:
                    act.wait_ge(made_done, q + NB)
                    act.wait_ge(rstd_ready, q)
                    act.wait_ge(g_lo_ready, q + (NB - 1))
                    for t in range(IT):
                        ins = nc.scalar.activation(nat[:, t, :], made[:, t, :], ACT.Identity,
                                                   bias=nmean[:, t:t + 1])
                    ins.then_inc(centred, 1)
                    act.wait_ge(centred, q - NB)
                    for t in range(IT):
                        ins = nc.scalar.activation(nat[:, t, :], nat[:, t, :], ACT.Relu,
                                                   scale=rstd[:, t:t + 1])
                    ins.then_inc(scaled, 1)
                    act.wait_ge(scaled, q - NB)
                    g_from(nat[:, :, :], g_hi[0], b, q + NB)

            def after_counts(c, q, dest, b):
                if c == COUNT_TAKE:
                    act.wait_ge(cols_done, q)
                    nc.scalar.activation(dest[:, tiles(b)], turned[:, 0, 0:IT], ACT.Copy).then_inc(cols_taken, 1)

            def take_row(number):
                act.wait_ge(row_turned, number)
                if number > 1:
                    act.wait_ge(row_stored, 16 * (number - 1))
                nc.scalar.activation(row[:, :], turned[0:N // P, 0, 0:P], ACT.Copy).then_inc(row_ready, 1)

            def one(q, layer, b, half):
                for c in range(NC):
                    if layer == HYPER:
                        act.wait_ge(inc_ready, (q - 2 * NB) * NC + (c + 1))
                    else:
                        act.wait_ge(raw_full[c % RING], q * (16 * NC // RING) + 16 * (c // RING + 1))
                    if not (is_first(q) and c < SPLIT):
                        act.wait_ge(chunk_done, q * NC + (c - SPLIT + 1))
                    nc.scalar.activation(hi[:, c % SPLIT, :], raw[:, c % RING, :], ACT.Copy).then_inc(hi_ready, 1)
                    if not is_first(q):
                        was, last_b = before(q, layer, b)
                        if was == GRAPH_1:
                            after_graph_1(c, q, last_b, 1 - half)
                            after_counts(c, q, cnt, last_b)
                        if was == GRAPH_2:
                            after_graph_2(c, q, last_b, 1 - half)
                            after_counts(c, q, rsum, last_b)
                    if is_at(q, NB) and c == NC - 1:
                        act.wait_ge(cols_step, 1)
                        nc.scalar.activation(col_b[:, :], col_a[:, :], ACT.Sqrt).then_inc(norm_root, 1)
                    if is_at(q, NB + 1) and c == 3:
                        take_row(1)
                    if is_at(q, 2 * NB + 1) and c == 3:
                        take_row(2)

            blocks(act, one)

        @block.vector
        def _(dve):
            def lo_of(dest, value, high, relu=False):
                if relu:
                    return nc.vector.scalar_tensor_tensor(out=dest, in0=value, scalar=0.0, in1=high.bitcast(f32),
                                                          op0=ALU.max, op1=ALU.subtract)
                return nc.vector.tensor_tensor(dest, value, high.bitcast(f32), ALU.subtract)

            def split_w(n):
                dve.wait_ge(w_hi_ready, n + 1)
                lo_of(w_lo[:, W_ORDER[n][1], :, :], xblk[:, 0, :].rearrange("p (k d) -> p k d", k=K),
                      w_hi[:, W_ORDER[n][1], :, :]).then_inc(w_lo_ready, 1)

            def ln_stats(source, n):
                step = (n - 1) * LN_STEPS
                if not is_at(n, 1):
                    dve.wait_ge(rstd_ready, n - 1)
                for t in range(IT):
                    ins = nc.vector.bn_stats(stats[:, t, :], source[:, t, :])
                ins.then_inc(ln_step, 1)
                dve.wait_ge(ln_step, step + 1)
                dve.sem_inc(stats_seen, 1)
                for t in range(IT):
                    ins = nc.vector.bn_aggr(mv[:, t, :], stats[:, t, :])
                ins.then_inc(ln_step, 1)
                dve.wait_ge(ln_step, step + 2)
                nc.vector.tensor_scalar(nmean[:, :], mv[:, :, 0], -1.0, None, ALU.mult)
                nc.vector.tensor_scalar(var[:, :], mv[:, :, 1], LN_EPS, None, ALU.add).then_inc(var_ready, 1)

            def ln_rstd(n):
                step = (n - 1) * LN_STEPS
                dve.wait_ge(root_ready, n)
                nc.vector.reciprocal(quot[:, :], root[:, :]).then_inc(ln_step, 1)
                dve.wait_ge(ln_step, step + 3)
                nc.vector.tensor_tensor(quot[:, :], quot[:, :], var[:, :], ALU.mult).then_inc(ln_step, 1)
                dve.wait_ge(ln_step, step + 4)
                nc.vector.tensor_tensor(quot[:, :], quot[:, :], root[:, :], ALU.add).then_inc(ln_step, 1)
                dve.wait_ge(ln_step, step + 5)
                nc.vector.reciprocal(quot[:, :], quot[:, :]).then_inc(ln_step, 1)
                dve.wait_ge(ln_step, step + 6)
                nc.vector.tensor_scalar(rstd[:, :], quot[:, :], 2.0, None, ALU.mult).then_inc(rstd_ready, 1)

            def h_lo(number):
                dve.wait_ge(h_hi_ready, number)
                lo_of(h_new[:, LO, :, :], turned[:, :, :], h_new[:, HI, :, :], relu=True).then_inc(h_lo_ready, 1)

            def g_lo_of_made(dest, high, b, number):
                dve.wait_ge(g_hi_ready, number)
                lo_of(dest[:, tiles(b), :], made[:, :, :], high[:, tiles(b), :]).then_inc(g_lo_ready, 1)

            def head(b, half):
                if isinstance(b, int):
                    dve.wait_ge(x_loaded[half], 16)
                else:
                    dve.wait_ge(x_loaded[half], (b - half) * 8 + 16)
                ln_stats(rows_in[half], b + 1)
                if not is_at(b, 0):
                    h_lo(b)
                ln_rstd(b + 1)
                dve.wait_ge(rstd_ready, b + 1)
                for t in range(IT):
                    ins = nc.vector.tensor_scalar(rows_in[half][:, t, :], rows_in[half][:, t, :],
                                                  nmean[:, t:t + 1], rstd[:, t:t + 1], ALU.add, ALU.mult)
                ins.then_inc(rows_ready, 1)
                if not is_at(b, 0):
                    g_lo_of_made(g_lo[0], g_hi[0], b - 1, b)

            for n in range(3):
                split_w(n)
            pairs(dve, head)
            h_lo(NB)
            g_lo_of_made(g_lo[0], g_hi[0], NB - 1, NB)
            split_w(3)
            dve.wait_ge(turned_done, NB)

            def sum_chunk(q, layer, c):
                chunk = raw[:, c % RING, :]
                if not (is_first(q) and c == 0):
                    dve.wait_ge(acc_step, q * NC + c)
                dest = acc[:, :]
                if c == NC - 1:
                    dest = acc_end[:, :]
                    if not is_first(q):
                        dve.wait_ge(cols_done, q)
                if layer == GRAPH_1 and c == 0:
                    ins = nc.vector.tensor_scalar(dest, chunk, 0.0, None, ALU.is_gt)
                elif layer == GRAPH_1:
                    ins = nc.vector.scalar_tensor_tensor(out=dest, in0=chunk, scalar=0.0, in1=acc[:, :],
                                                         op0=ALU.is_gt, op1=ALU.add)
                elif c == 0:
                    ins = nc.vector.tensor_copy(dest, chunk)
                else:
                    ins = nc.vector.tensor_tensor(dest, acc[:, :], chunk, ALU.add)
                ins.then_inc(acc_step, 1)

            def split_chunk(number, c):
                if not (isinstance(number, int) and number < SPLIT):
                    dve.wait_ge(chunk_done, number - (SPLIT - 1))
                dve.wait_ge(hi_ready, number + 1)
                lo_of(lo[:, c % SPLIT, :], raw[:, c % RING, :], hi[:, c % SPLIT, :]).then_inc(lo_ready, 1)

            def incidence(q, c, half):
                number = (q - 2 * NB) * NC + c
                chunk = raw[:, c % RING, :].rearrange("p (t n) -> p t n", t=CT)
                scale = rn_row[:, half, :].rearrange("p (a n) -> p a n", a=1).broadcast_to([P, CT, BW])
                if is_at(q, 2 * NB) and c == 0:
                    dve.wait_ge(acc_step, q * NC)
                else:
                    dve.wait_ge(inc_ready, number)
                nc.vector.scalar_tensor_tensor(out=acc_t, in0=chunk, scalar=0.0, in1=scale,
                                               op0=ALU.is_gt, op1=ALU.mult).then_inc(acc_step, 1)
                dve.wait_ge(acc_step, q * NC + (c + 1))
                nc.vector.tensor_tensor(chunk, chunk, acc_t, ALU.add).then_inc(inc_ready, 1)

            def after_graph_1(c, q, b, half):
                if c == TAKE:
                    dve.wait_ge(h_hi_ready, q + NB)
                    lo_of(h_new[:, LO, :, :], main[:, half, :, :], h_new[:, HI, :, :],
                          relu=True).then_inc(h_lo_ready, 1)
                if c == SPLIT_MADE:
                    g_lo_of_made(g_lo[1], g_hi[1], b, q + NB)

            def after_graph_2(c, q, b, half):
                if c == TAKE:
                    dve.wait_ge(chunk_done, q * NC)
                    dve.wait_ge(xblk_loaded, (q - NB) * 16)
                    nc.vector.scalar_tensor_tensor(out=xblk[:, :, :], in0=main[:, half, :, :], scalar=0.0,
                                                   in1=xblk[:, :, :], op0=ALU.max, op1=ALU.add
                                                   ).then_inc(xblk_ready, 1)
                if c == STATS:
                    dve.wait_ge(made_done, q + NB)
                    ln_stats(made, q)
                if c == NORM:
                    ln_rstd(q)
                if c == SPLIT_NORM:
                    dve.wait_ge(g_hi_ready, q + NB)
                    lo_of(g_lo[0][:, tiles(b), :], nat[:, :, :], g_hi[0][:, tiles(b), :]).then_inc(g_lo_ready, 1)

            def after_hyper(q, half):
                dve.wait_ge(chunk_done, q * NC)
                dve.wait_ge(rd_loaded, (q - 2 * NB) * 16)
                scale = rd_row[:, :].rearrange("p (a n) -> p a n", a=1).broadcast_to([P, K, BW])
                result = nat[:, :, :].rearrange("p t d -> p (t d)").rearrange("p (k n) -> p k n", k=K)
                nc.vector.tensor_tensor(result, main[:, half, :, :], scale, ALU.mult).then_inc(product, 1)
                dve.wait_ge(product, q - 2 * NB)
                dve.wait_ge(xblk_loaded, (q - NB) * 16)
                nc.vector.tensor_tensor(xblk[:, :, :], result, xblk[:, :, :], ALU.add).then_inc(xblk_ready, 1)

            def norms():
                dve.wait_ge(norm_root, 1)
                nc.vector.reciprocal(rn[:, :], col_b[:, :]).then_inc(cols_step, 1)
                dve.wait_ge(cols_step, 2)
                nc.vector.tensor_tensor(rn[:, :], rn[:, :], col_a[:, :], ALU.mult).then_inc(cols_step, 1)
                dve.wait_ge(cols_step, 3)
                nc.vector.tensor_tensor(rn[:, :], rn[:, :], col_b[:, :], ALU.add).then_inc(cols_step, 1)
                dve.wait_ge(cols_step, 4)
                nc.vector.tensor_scalar(rn[:, :], rn[:, :], 0.5, NORM_EPS, ALU.mult, ALU.max).then_inc(cols_step, 1)
                dve.wait_ge(cols_step, 5)
                nc.vector.reciprocal(rn[:, :], rn[:, :]).then_inc(cols_step, 1)

            def degrees():
                dve.wait_ge(cols_taken, 2 * NB)
                nc.vector.tensor_tensor(col_a[:, :], cnt[:, :], rn[:, :], ALU.mult).then_inc(cols_step, 1)
                dve.wait_ge(cols_step, 7)
                nc.vector.tensor_tensor(col_a[:, :], col_a[:, :], rsum[:, :], ALU.add).then_inc(cols_step, 1)
                dve.wait_ge(cols_step, 8)
                nc.vector.reciprocal(rdeg[:, :], col_a[:, :]).then_inc(cols_step, 1)

            def one(q, layer, b, half):
                for c in range(NC):
                    dve.wait_ge(raw_full[c % RING], q * (16 * NC // RING) + 16 * (c // RING + 1))
                    if layer == HYPER:
                        if c == 0:
                            loads = 1 if isinstance(b, int) else None
                            if loads:
                                dve.wait_ge(rn_loaded[half], 16)
                            else:
                                dve.wait_ge(rn_loaded[half], (b - half) * 8 + 16)
                        incidence(q, c, half)
                        if not (is_at(q, 2 * NB) and c == 0):
                            split_chunk(q * NC + (c - 1), (c - 1) % NC)
                    else:
                        sum_chunk(q, layer, c)
                        split_chunk(q * NC + c, c)
                    if not is_first(q):
                        was, last_b = before(q, layer, b)
                        if was == GRAPH_1:
                            after_graph_1(c, q, last_b, 1 - half)
                        if was == GRAPH_2:
                            after_graph_2(c, q, last_b, 1 - half)
                        if was == HYPER and c == FINISH:
                            after_hyper(q, 1 - half)
                    if is_at(q, NB) and c == NC - 2:
                        dve.wait_ge(cols_taken, NB)
                        nc.vector.tensor_scalar(col_a[:, :], cnt[:, :], NORM_EPS * NORM_EPS, None,
                                                ALU.max).then_inc(cols_step, 1)
                    if is_at(q, NB) and c == NC - 1:
                        norms()
                    if is_at(q, 2 * NB) and c == NC - 1:
                        degrees()

            blocks(dve, one)
            split_chunk(3 * NB * NC - 1, NC - 1)
            after_hyper(3 * NB, 1)

        @block.tensor
        def _(pe):
            def three(dest, stationary, moving, start, stop):
                nc.tensor.matmul(dest, stationary[HI], moving[HI], start=start, stop=False)
                nc.tensor.matmul(dest, stationary[LO], moving[HI], start=False, stop=False)
                return nc.tensor.matmul(dest, stationary[HI], moving[LO], start=False, stop=stop)

            def times_wb():
                for t in range(IT):
                    for k in range(K):
                        h = [h_new[:, s, k, t * P:(t + 1) * P] for s in (HI, LO)]
                        ins = three(made[:, t, :], h, (w_hi[:, WB, k, :], w_lo[:, WB, k, :]), k == 0, k == K - 1)
                ins.then_inc(made_done, 1)

            def turn(b, half):
                pe.wait_ge(rows_ready, b + 1)
                for t in range(IT):
                    for k in range(K):
                        ins = nc.tensor.transpose(turned[:, k, t * P:(t + 1) * P],
                                                  rows_in[half][:, t, k * P:(k + 1) * P], ident[:, :])
                ins.then_inc(turned_done, 1)

            def head(b, half):
                if not is_at(b, 0):
                    pe.wait_ge(h_lo_ready, b)
                    if not is_at(b, 1):
                        pe.wait_ge(g_lo_ready, b - 1)
                    times_wb()
                turn(b, half)

            pe.wait_ge(const_step, 3)
            pe.wait_ge(w_lo_ready, 3)
            pairs(pe, head)
            pe.wait_ge(h_lo_ready, NB)
            pe.wait_ge(g_lo_ready, NB - 1)
            times_wb()

            def times_wa(q, layer, half):
                pe.wait_ge(h_loaded, (q + 1) * 16)
                place = (WA_1, WA_2)[layer]
                for f in range(K):
                    for k in range(K):
                        weight = [m[:, place, k, f * P:(f + 1) * P] for m in (w_hi, w_lo)]
                        ins = three(main[:, half, f, :], weight, [h_old[:, s, k, :] for s in (HI, LO)],
                                    k == 0, False)
                ins.then_inc(h_used, 1)

            def made_free(number):
                pe.wait_ge(g_hi_ready, number - 1)
                pe.wait_ge(g_lo_ready, number - 1)

            def sum_columns(q):
                pe.wait_ge(acc_step, q * NC)
                if not is_at(q, 1):
                    pe.wait_ge(cols_taken, q - 1)
                if is_at(q, NB + 1):
                    pe.wait_ge(row_ready, 1)
                for t in range(IT):
                    for s in range(CT):
                        ins = nc.tensor.matmul(turned[:, 0, t:t + 1], acc_end[:, s * BW + t * P:s * BW + (t + 1) * P],
                                               ones[:, :], start=s == 0, stop=s == CT - 1)
                ins.then_inc(cols_done, 1)

            def turn_cols(source, step, number):
                pe.wait_ge(cols_step, step)
                pe.wait_ge(cols_taken, number * NB)
                nc.tensor.transpose(turned[0:N // P, 0, 0:P], source[:, :], ident[:, :]).then_inc(row_turned, 1)

            def after_graph_1(c, q):
                if c == MAKE:
                    if is_at(q, 1):
                        pe.wait_ge(w_lo_ready, 4)
                    pe.wait_ge(h_lo_ready, q + NB)
                    made_free(q + NB)
                    times_wb()

            def after_graph_2(c, q):
                if c == MAKE:
                    pe.wait_ge(xblk_ready, q - NB)
                    made_free(q + NB)
                    for t in range(IT):
                        for k in range(K):
                            ins = nc.tensor.transpose(made[:, t, k * P:(k + 1) * P],
                                                      xblk[:, k, t * P:(t + 1) * P], ident[:, :])
                    ins.then_inc(made_done, 1)

            def one(q, layer, b, half):
                if layer == GRAPH_1 and is_first(q):
                    pe.wait_ge(g_lo_ready, NB)
                elif not (isinstance(q, int) and q < 2):
                    if layer == GRAPH_1 or is_at(q, NB) or is_at(q, NB + 1):
                        pe.wait_ge(h_lo_ready, q + (NB - 1))
                    else:
                        pe.wait_ge(xblk_ready, q - (NB + 1))
                if isinstance(b, int) and b == 0 and layer:
                    pe.wait_ge(g_lo_ready, (layer + 1) * NB - 1)
                if layer != HYPER:
                    times_wa(q, layer, half)
                at = layer % 2
                for c in range(NC):
                    if isinstance(b, int) and b == 0 and layer and c * CT == (NB - 1) * IT:
                        pe.wait_ge(g_lo_ready, (layer + 1) * NB)
                    pe.wait_ge(hi_ready, q * NC + (c + 1))
                    pe.wait_ge(lo_ready, q * NC + (c + 1))
                    for s in range(CT):
                        j = c * CT + s
                        for f in range(K):
                            g = [m[at][:, j, f * P:(f + 1) * P] for m in (g_hi, g_lo)]
                            ins = three(main[:, half, f, :], g,
                                        [m[:, c % SPLIT, s * BW:(s + 1) * BW] for m in (hi, lo)],
                                        layer == HYPER and j == 0, j == N // P - 1)
                    ins.then_inc(chunk_done, 1)
                    if not is_first(q):
                        was, last_b = before(q, layer, b)
                        if was == GRAPH_1:
                            after_graph_1(c, q)
                        if was == GRAPH_2:
                            after_graph_2(c, q)
                        if was != HYPER and c == COUNT:
                            sum_columns(q)
                    if is_at(q, NB + 1) and c == 1:
                        turn_cols(rn, 6, 1)
                    if is_at(q, 2 * NB + 1) and c == 1:
                        turn_cols(rdeg, 9, 2)

            blocks(pe, one)


def kernel(x, adj, L0_gnn_W1, L0_gnn_W2):
    import numpy as np
    import concourse.bacc as bacc
    from concourse.bass_utils import run_bass_kernel_spmd

    x, adj, w1, w2 = (np.asarray(a) for a in (x, adj, L0_gnn_W1, L0_gnn_W2))
    f32, f32r = mybir.dt.float32, mybir.dt.float32r
    arrays = {
        "adj_t": adj.reshape(NB, BW, NC, CT, P).transpose(0, 2, 4, 3, 1).reshape(NB, NC, P, CW),
        "x_rows": x.reshape(NB, IT, P, D).transpose(0, 2, 1, 3),
        "x_cols": x.reshape(NB, BW, K, P).transpose(0, 3, 2, 1).reshape(NB, P, K * BW),
        "w": np.stack([w1, w2]).reshape(4, K, P, D).transpose(0, 2, 1, 3).reshape(4, P, K * D),
    }
    arrays = {name: np.ascontiguousarray(a) for name, a in arrays.items()}
    nc = bacc.Bacc("TRN2", target_bir_lowering=False, num_devices=1)
    ins = [nc.dram_tensor(name, a.shape, f32, kind="ExternalInput").ap() for name, a in arrays.items()]
    out = nc.dram_tensor("out", (NB, P, K * BW), f32, kind="ExternalOutput").ap()
    h_mem = nc.dram_tensor("h_mem", (2, NB, P, 2 * K * BW), f32r, kind="Internal").ap()
    x1_mem = nc.dram_tensor("x1_mem", (NB, P, K * BW), f32, kind="Internal").ap()
    rn_mem = nc.dram_tensor("rn_mem", (NB, BW), f32, kind="Internal").ap()
    rd_mem = nc.dram_tensor("rd_mem", (NB, BW), f32, kind="Internal").ap()
    gnn_kernel(nc, *ins, out, h_mem, x1_mem, rn_mem, rd_mem)
    result = run_bass_kernel_spmd(nc, [arrays], core_ids=[0]).results[0]["out"]
    return np.ascontiguousarray(result.reshape(NB, P, K, BW).transpose(0, 3, 2, 1)).reshape(N, D)
```

```python
import concourse.bass as bass
from concourse import mybir
from contextlib import ExitStack

P = 128
N = 4096
D = 256
K = D // P
BW = 512
NB = N // BW
IT = BW // P
CT = 2
CW = CT * BW
NC = N // (P * CT)
RING, RING_MORE = 4, 4
HI_RING = 4
LO_RING, LO_MORE = 2, 2
LN_EPS = 1e-5
NORM_EPS = 1e-12
GRAPH_1, GRAPH_2, HYPER = range(3)
WA_1, WB, WA_2 = range(3)
HI, LO = range(2)

WHOLE = range(1, NC, 2)
WHOLE_FIRST = range(NC // 2 - 1, NC - 2, 2)

TAKE = 1
MAKE = 3
SPLIT_MADE, SPLIT_MADE_HI = 5, 7
STATS, ROOT, RSTD = 5, 7, 7
NORM, SPLIT_NORM = 9, 9
WA_AT = (4, 9)
FOLD = 2
COUNT, COUNT_TAKE = 10, 14
FINISH = 9
LN_STEPS = 6
LN_HEAD = NB // 2


def gnn_kernel(nc, adj_t, x_rows, x_cols, w, out, h_mem, g_mem, x1_mem, rn_mem, rd_mem):
    f32, f32r = mybir.dt.float32, mybir.dt.float32r
    ALU, ACT = mybir.AluOpType, mybir.ActivationFunctionType

    with ExitStack() as ctx:
        def sb(name, shape, dt=f32, where=ctx):
            return where.enter_context(nc.sbuf_tensor(name, shape, dt))

        def sem(name):
            return ctx.enter_context(nc.semaphore(name))

        with ExitStack() as graph_only:
            g_lo_1 = sb("g_lo1", [P, N // P, D], f32r, graph_only)
        raw_more = sb("raw_more", [P, RING_MORE, CW])
        lo_more = sb("lo_more", [P, LO_MORE, CW], f32r)
        step_more = sb("step_more", [P, CW])
        rd_row = sb("rd_row", [P, CW])
        g_lo = [sb("g_lo0", [P, N // P, D], f32r), g_lo_1]
        with ExitStack() as head_only:
            x_all = sb("x_all", [P, NB, IT, D], f32, head_only)
        with ExitStack() as graph_only:
            g_hi_1 = sb("g_hi1", [P, N // P, D], f32r, graph_only)
        g_whole = sb("g_whole", [P, N // P, D])
        g_hi = [sb("g_hi0", [P, N // P, D], f32r), g_hi_1]
        raw = sb("raw", [P, RING, CW])
        hi = sb("hi", [P, HI_RING, CW], f32r)
        lo = sb("lo", [P, LO_RING, CW], f32r)
        w_hi = sb("w_hi", [P, 3, K, D], f32r)
        w_lo = sb("w_lo", [P, 3, K, D], f32r)
        xblk = sb("xblk", [P, K, BW])
        nat = sb("nat", [P, IT, D])
        acc = sb("acc", [P, CW])
        ident = sb("ident", [P, P])
        ones = sb("ones", [P, 2])
        ones_r = sb("ones_r", [P, 2], f32r)
        stats = sb("stats", [P, 2 * IT, 6])
        mv = sb("mv", [P, 2 * IT, 2])
        nmean2 = sb("nmean2", [P, 2 * IT])
        var = sb("var", [P, 2 * IT])
        root = sb("root", [P, 2 * IT])
        quot = sb("quot", [P, 2 * IT])
        rstd = sb("rstd", [P, 2 * IT])
        shift = sb("shift", [P, 2 * IT])
        cnt = sb("cnt", [P, N // P])
        rsum = sb("rsum", [P, N // P])
        col_a = sb("col_a", [P, N // P])
        col_b = sb("col_b", [P, N // P])
        rn = sb("rn", [P, N // P])
        rdeg = sb("rdeg", [P, N // P])
        h_old = sb("h_old", [P, 2, BW], f32r)
        with ExitStack() as early:
            h_new = sb("h_new", [P, 2, K, BW], f32r, early)
            count_fold = sb("count_fold", [P, BW], f32r, early)
        rn_row = sb("rn_row", [P, 2, BW])
        acc_late = sb("acc_late", [P, CW])
        row = sb("row", [N // P, 4 * P])
        acc_end = [nat[:, :, :].rearrange("p t d -> p (t d)"), acc_late[:, :]]
        folded = [count_fold[:, :], acc_late[:, 0:BW]]

        main = ctx.enter_context(nc.psum_tensor("main", [P, 2, K, BW], f32))
        turned = ctx.enter_context(nc.psum_tensor("turned", [P, K, BW], f32))
        made = ctx.enter_context(nc.psum_tensor("made", [P, IT, D], f32))

        turned_of = [turned[:, :, :], main[:, 0, :, :]]
        made_of = [made[:, :, :], main[:, 1, :, :].rearrange("p k (t d) -> p (k t) d", d=D)]

        raw_full = [sem(f"raw_full{r}") for r in range(RING + RING_MORE)]
        inc_ready = sem("inc_ready")
        hi_ready = sem("hi_ready")
        lo_ready = sem("lo_ready")
        acc_step = sem("acc_step")
        fold_ready = sem("fold_ready")
        chunk_done = sem("chunk_done")
        h_hi_ready = sem("h_hi_ready")
        h_lo_ready = sem("h_lo_ready")
        h_stored = sem("h_stored")
        h_loaded = sem("h_loaded")
        h_used = sem("h_used")
        turned_done = sem("turned_done")
        head_stored = [sem(f"head_stored{s}") for s in range(2)]
        w_read = sem("w_read")
        made_done = sem("made_done")
        g_hi_ready = sem("g_hi_ready")
        g_lo_ready = sem("g_lo_ready")
        x_loaded = [sem(f"x_loaded{i}") for i in range(LN_HEAD)]
        normed = sem("normed")
        g_stored = sem("g_stored")
        g_loaded = [sem(f"g_loaded{b}") for b in range(NB)]
        xblk_loaded = sem("xblk_loaded")
        xblk_ready = sem("xblk_ready")
        xblk_stored = sem("xblk_stored")
        out_stored = sem("out_stored")
        ln_step = sem("ln_step")
        quot_ready = sem("quot_ready")
        var_ready = sem("var_ready")
        root_ready = sem("root_ready")
        rstd_ready = sem("rstd_ready")
        w_loaded = [sem(f"w_loaded{n}") for n in range(4)]
        w_hi_ready = sem("w_hi_ready")
        w_lo_ready = sem("w_lo_ready")
        cols_done = sem("cols_done")
        cols_taken = sem("cols_taken")
        cols_step = sem("cols_step")
        norm_root = sem("norm_root")
        row_turned = sem("row_turned")
        row_ready = sem("row_ready")
        row_stored = sem("row_stored")
        rn_loaded = [sem(f"rn_loaded{s}") for s in range(2)]
        rd_loaded = sem("rd_loaded")
        product = sem("product")
        const_step = sem("const_step")
        ones_ready = sem("ones_ready")
        stats_seen = sem("stats_seen")
        block_seen = sem("block_seen")

        block = ctx.enter_context(nc.Block())

        def blocks(eng, one):
            for layer in (GRAPH_1, GRAPH_2, HYPER):
                for b in range(2):
                    one(NB * layer + b, layer, b, b)
                with eng.Fori(1, NB // 2) as pair:
                    for half in range(2):
                        b = 2 * pair + half
                        one(b + NB * layer, layer, b, half)

        def is_first(q):
            return isinstance(q, int) and q == 0

        def is_at(q, number):
            return isinstance(q, int) and q == number

        def before(q, layer, b):
            if isinstance(b, int) and b == 0:
                return layer - 1, NB - 1
            return layer, b - 1

        def tiles(b):
            return bass.ds(b * IT, IT)

        W_ORDER = [(1, WB), (0, WA_1), (2, WA_2), (3, WB)]
        w_raw = [xblk[:, n, :].rearrange("p (k d) -> p k d", k=K) for n in range(2)]
        w_raw += [nat[:, 2 * n:2 * n + 2, :] for n in range(2)]

        def whole(q, layer, c):
            return layer == HYPER and c in (WHOLE_FIRST if is_at(q, 2 * NB) else WHOLE)

        def split_list(q, layer):
            return [c for c in range(NC) if not whole(q, layer, c)]

        def splits(q, layer, c):
            here = sum(not whole(q, layer, a) for a in range(c))
            if layer != HYPER or is_at(q, 2 * NB):
                return q * NC + here
            return (q - (2 * NB + 1)) * (NC - len(WHOLE)) + (2 * NB + 1) * NC - len(WHOLE_FIRST) + here

        def chunk_before(q, layer, c, back):
            if c >= back:
                return q, layer, c - back
            return q - 1, before(q, layer, b_of(q, layer))[0], c - back + NC

        def b_of(q, layer):
            return q - NB * layer

        def ring_of(layer):
            return RING + RING_MORE if layer == HYPER else RING

        def raw_at(layer, c):
            r = c % ring_of(layer)
            return raw[:, r, :] if r < RING else raw_more[:, r - RING, :]

        def wait_raw(eng, q, layer, c):
            ring = ring_of(layer)
            loads = 16 * (c // ring + 1)
            if layer != HYPER:
                eng.wait_ge(raw_full[c % ring], q * (16 * NC // ring) + loads)
            else:
                if c % ring < RING:
                    loads += 2 * NB * (16 * NC // RING)
                eng.wait_ge(raw_full[c % ring], (q - 2 * NB) * (16 * NC // ring) + loads)

        def lo_ring(layer):
            return LO_RING + LO_MORE if layer == HYPER else LO_RING

        def lo_at(q, layer, c):
            r = slot(q, layer, c, lo_ring(layer))
            return lo[:, r, :] if r < LO_RING else lo_more[:, r - LO_RING, :]

        def lo_free(q, layer, c):
            n = split_list(q, layer).index(c)
            if is_at(q, 2 * NB) and n < LO_RING:
                return last_of_slot(q, layer, c, LO_RING)
            if is_at(q, 2 * NB) and n < LO_RING + LO_MORE:
                return q * NC
            return last_of_slot(q, layer, c, lo_ring(layer))

        def last_of_slot(q, layer, c, ring):
            n = split_list(q, layer).index(c) - ring
            if n >= 0:
                return q * NC + (split_list(q, layer)[n] + 1)
            was = before(q, layer, b_of(q, layer))[0]
            return (q - 1) * NC + (split_list(q - 1, was)[n] + 1)

        def slot(q, layer, c, ring):
            return split_list(q, layer).index(c) % ring

        @block.sync
        def _(sp):
            def load_chunk(layer, b, c):
                sp.dma_start(raw_at(layer, c), adj_t[b, c, :, :]).then_inc(raw_full[c % ring_of(layer)], 16)

            for i in range(LN_HEAD):
                sp.dma_start(x_all[:, 2 * i:2 * i + 2, :, :], x_rows[2 * i:2 * i + 2, :, :, :].rearrange(
                    "b p t d -> p b t d")).then_inc(x_loaded[i], 16)
            for c in range(RING):
                load_chunk(GRAPH_1, 0, c)
            for b in range(NB):
                sp.wait_ge(h_hi_ready, b + 1)
                sp.dma_start(h_mem[GRAPH_1, b, :, :, HI, :].rearrange("k p n -> p k n"),
                             hi[:, b % 2, :].bitcast(f32).rearrange("p (k n) -> p k n", k=K)).then_inc(head_stored[b % 2], 16)
                sp.wait_ge(h_lo_ready, b + 1)
                sp.dma_start(h_mem[GRAPH_1, b, :, :, LO, :].rearrange("k p n -> p k n"),
                             lo[:, b % 2, :].bitcast(f32).rearrange("p (k n) -> p k n", k=K)).then_inc(head_stored[b % 2], 16)

            def one(q, layer, b, half):
                for c in range(NC):
                    if is_first(q) and c < RING:
                        continue
                    new = is_at(q, 2 * NB) and RING <= c < RING + RING_MORE
                    back = RING if is_at(q, 2 * NB) and c < RING else ring_of(layer)
                    old_q, old_layer, old_c = chunk_before(q, layer, c, back)
                    if new:
                        sp.wait_ge(chunk_done, q * NC)
                    elif whole(old_q, old_layer, old_c):
                        sp.wait_ge(chunk_done, old_q * NC + (old_c + 1))
                    else:
                        sp.wait_ge(hi_ready, splits(old_q, old_layer, old_c + 1))
                        sp.wait_ge(lo_ready, splits(old_q, old_layer, old_c + 1))
                    load_chunk(layer, b, c)

            blocks(sp, one)

        @block.gpsimd
        def _(pool):
            for n in range(4):
                pool.dma_start(w_raw[n], w[W_ORDER[n][0], :, :, :]).then_inc(w_loaded[n], 16)
            nc.gpsimd.memset(ident[:, :], 0.0).then_inc(const_step, 1)
            nc.gpsimd.memset(ones[:, :], 1.0).then_inc(const_step, 1)
            pool.wait_ge(const_step, 2)
            nc.gpsimd.affine_select(out=ident[:, :], in_=ident[:, :], compare_op=ALU.not_equal, fill=1.0,
                                    base=0, pattern=[[-1, P]], channel_multiplier=1).then_inc(const_step, 1)

            def load_h(q, layer, b, k):
                if not (is_first(q) and k == 0):
                    pool.wait_ge(h_used, q * K + k)
                pool.dma_start(h_old[:, :, :].bitcast(f32), h_mem[layer, b, k, :, :, :]).then_inc(h_loaded, 16)

            def store_h(q):
                pool.wait_ge(h_hi_ready, q + NB)
                pool.wait_ge(h_lo_ready, q + NB)
                pool.dma_start(h_mem[GRAPH_2, q - 1, :, :, :, :].rearrange("k p s n -> p s k n"),
                               h_new[:, :, :, :].bitcast(f32)).then_inc(h_stored, 16)
                pool.wait_ge(h_stored, q * 16)

            def load_xblk(source):
                pool.dma_start(xblk[:, :, :].rearrange("p k n -> p (k n)"), source).then_inc(xblk_loaded, 16)

            def load_x_cols(b):
                if not is_at(b, 0):
                    pool.wait_ge(made_done, b + 2 * NB)
                load_xblk(x_cols[b, :, :])

            def store_x1(b):
                pool.wait_ge(xblk_ready, b + 1)
                pool.sem_inc(block_seen, 1)
                pool.dma_start(x1_mem[b, :, :], xblk[:, :, :].rearrange("p k n -> p (k n)")
                               ).then_inc(xblk_stored, 16)
                pool.wait_ge(xblk_stored, (b + 1) * 16)

            def store_g(b):
                pool.wait_ge(normed, b + (NB + 1))
                pool.sem_inc(block_seen, 1)
                pool.dma_start(g_mem[b, :, :, :], nat[:, :, :]).then_inc(g_stored, 16)
                pool.wait_ge(g_stored, (b + 1) * 16)

            def spread(dest, mem, b, done):
                pool.dma_start(dest, mem[bass.ds(b, 1), :].partition_broadcast(P)).then_inc(done, 16)

            def store_row(number, mem):
                pool.wait_ge(row_ready, number)
                pool.dma_start(mem.rearrange("b (t p) -> (b t) p", p=P), row[:, 0:P]).then_inc(row_stored, 16)
                pool.wait_ge(row_stored, number * 16)

            for half in range(2):
                pool.wait_ge(head_stored[half], 32 * NB // 2)
            load_h(0, GRAPH_1, 0, 0)
            load_h(0, GRAPH_1, 0, 1)
            load_h(1, GRAPH_1, 1, 0)
            with pool.Fori(1, NB - 1) as q:
                load_h(q, GRAPH_1, q, 1)
                store_h(q)
                load_h(q + 1, GRAPH_1, q + 1, 0)
            load_h(NB - 1, GRAPH_1, NB - 1, 1)
            store_h(NB - 1)
            load_h(NB, GRAPH_2, 0, 0)

            load_h(NB, GRAPH_2, 0, 1)
            load_x_cols(0)
            store_h(NB)
            load_h(NB + 1, GRAPH_2, 1, 0)
            load_h(NB + 1, GRAPH_2, 1, 1)
            store_x1(0)
            store_row(1, rn_mem)
            for half in range(2):
                spread(rn_row[:, half, :], rn_mem, half, rn_loaded[half])
            store_g(0)
            load_h(NB + 2, GRAPH_2, 2, 0)
            with pool.Fori(2, NB - 1) as b:
                load_x_cols(b - 1)
                load_h(b + NB, GRAPH_2, b, 1)
                store_x1(b - 1)
                store_g(b - 1)
                load_h(b + (NB + 1), GRAPH_2, b + 1, 0)
            load_x_cols(NB - 2)
            load_h(2 * NB - 1, GRAPH_2, NB - 1, 1)
            store_x1(NB - 2)
            store_g(NB - 2)

            def load_g(b):
                pool.dma_start(g_whole[:, b * IT:(b + 1) * IT, :], g_mem[b, :, :, :]).then_inc(g_loaded[b], 16)

            load_x_cols(NB - 1)
            pool.wait_ge(chunk_done, 2 * NB * NC)
            for b in range(NB // 2 - 1, NB - 1):
                load_g(b)
            store_x1(NB - 1)
            for b in range(NB // 2 - 1):
                load_g(b)
            store_g(NB - 1)
            load_g(NB - 1)
            store_row(2, rd_mem)
            pool.wait_ge(made_done, 3 * NB)

            def last(b, half, more):
                load_xblk(x1_mem[b, :, :])
                spread(rd_row[:, 0:BW], rd_mem, b, rd_loaded)
                if more:
                    pool.wait_ge(inc_ready, b * NC + NC)
                    spread(rn_row[:, half, :], rn_mem, b + 2, rn_loaded[half])
                pool.wait_ge(xblk_ready, b + (NB + 1))
                pool.sem_inc(block_seen, 1)
                pool.dma_start(out[b, :, :], xblk[:, :, :].rearrange("p k n -> p (k n)")
                               ).then_inc(out_stored, 16)
                pool.wait_ge(out_stored, b * 16 + 16)

            with pool.Fori(0, NB // 2 - 1) as pair:
                for half in range(2):
                    last(2 * pair + half, half, True)
            for half in range(2):
                last(NB - 2 + half, half, False)

        @block.scalar
        def _(act):
            def split_w(n):
                act.wait_ge(w_loaded[n], 16)
                if n == 3:
                    act.wait_ge(made_done, NB)
                nc.scalar.activation(w_hi[:, W_ORDER[n][1], :, :], w_raw[n], ACT.Copy).then_inc(w_hi_ready, 1)

            def ln_root(n, width):
                act.wait_ge(var_ready, n)
                nc.scalar.activation(root[:, 0:width], var[:, 0:width], ACT.Sqrt).then_inc(root_ready, 1)

            def g_hi_from(source, dest, b):
                nc.scalar.activation(dest[:, tiles(b), :], source, ACT.Copy).then_inc(g_hi_ready, 1)

            def head_norm(i):
                ln_root(i + 1, 2 * IT)
                act.wait_ge(rstd_ready, i + 1)
                for b in range(2):
                    for t in range(IT):
                        n = b * IT + t
                        ins = nc.scalar.activation(x_all[:, 2 * i + b, t, :], x_all[:, 2 * i + b, t, :], ACT.Relu,
                                                   bias=shift[:, n:n + 1], scale=rstd[:, n:n + 1])
                    ins.then_inc(normed, 1)

            def head_h(b):
                act.wait_ge(turned_done, b + 1)
                if b >= 2:
                    act.wait_ge(head_stored[b % 2], 32 * (b // 2))
                    act.wait_ge(made_done, b - 1)
                nc.scalar.activation(hi[:, b % 2, :], turned_of[b % 2], ACT.Copy).then_inc(h_hi_ready, 1)

            def head_g(b):
                act.wait_ge(made_done, b + 1)
                g_hi_from(made_of[b % 2], g_hi[0], b)

            act.wait_ge(const_step, 2)
            nc.scalar.activation(ones_r[:, :], ones[:, :], ACT.Copy).then_inc(ones_ready, 1)
            split_w(0)
            head_norm(0)
            split_w(1)
            split_w(2)
            for i in range(LN_HEAD):
                head_h(2 * i)
                head_h(2 * i + 1)
                if i + 1 < LN_HEAD:
                    head_norm(i + 1)
                head_g(2 * i)
                head_g(2 * i + 1)
            split_w(3)
            for half in range(2):
                act.wait_ge(head_stored[half], 32 * NB // 2)

            def after_graph_1(c, q, b, half):
                if c == TAKE:
                    act.wait_ge(chunk_done, q * NC)
                    if not is_at(q, 1):
                        act.wait_ge(h_stored, (q - 1) * 16)
                        act.wait_ge(made_done, q + (NB - 1))
                    nc.scalar.activation(h_new[:, HI, :, :], main[:, half, :, :], ACT.Relu).then_inc(h_hi_ready, 1)
                if c == SPLIT_MADE_HI:
                    act.wait_ge(made_done, q + NB)
                    g_hi_from(made[:, :, :], g_hi[1], b)

            def after_graph_2(c, q, b, half):
                if c == ROOT:
                    ln_root(q - NB + LN_HEAD, IT)
                if c == NORM:
                    act.wait_ge(rstd_ready, q - NB + LN_HEAD)
                    if is_at(q, NB + 1):
                        act.wait_ge(cols_done, NB)
                    else:
                        act.wait_ge(g_lo_ready, q + (NB - 1))
                        act.wait_ge(g_stored, (q - (NB + 1)) * 16)
                    for t in range(IT):
                        ins = nc.scalar.activation(nat[:, t, :], made[:, t, :], ACT.Relu,
                                                   bias=shift[:, t:t + 1], scale=rstd[:, t:t + 1])
                    ins.then_inc(normed, 1)
                    act.wait_ge(normed, q)
                    g_hi_from(nat[:, :, :], g_hi[0], b)

            def after_counts(c, q, dest, b):
                if c == COUNT_TAKE:
                    act.wait_ge(cols_done, q)
                    nc.scalar.activation(dest[:, tiles(b)], turned[:, 0, 0:2 * IT:2], ACT.Copy).then_inc(cols_taken, 1)

            def take_row(number):
                act.wait_ge(row_turned, number)
                if number > 1:
                    act.wait_ge(row_stored, 16 * (number - 1))
                nc.scalar.activation(row[:, 0:P], turned[0:N // P, 0, 0:P], ACT.Copy).then_inc(row_ready, 1)

            def split_chunk(q, layer, c):
                if layer == HYPER:
                    act.wait_ge(inc_ready, (q - 2 * NB) * NC + (c + 1))
                else:
                    wait_raw(act, q, layer, c)
                if not (is_first(q) and c < HI_RING):
                    act.wait_ge(chunk_done, last_of_slot(q, layer, c, HI_RING))
                nc.scalar.activation(hi[:, slot(q, layer, c, HI_RING), :], raw_at(layer, c), ACT.Copy
                                     ).then_inc(hi_ready, 1)

            def one(q, layer, b, half):
                for c in range(NC):
                    if not whole(q, layer, c):
                        split_chunk(q, layer, c)
                    if not is_first(q):
                        was, last_b = before(q, layer, b)
                        if was == GRAPH_1:
                            after_graph_1(c, q, last_b, 1 - half)
                            after_counts(c, q, cnt, last_b)
                        if was == GRAPH_2:
                            after_graph_2(c, q, last_b, 1 - half)
                            after_counts(c, q, rsum, last_b)
                    if is_at(q, NB) and c == NC - 1:
                        act.wait_ge(cols_step, 1)
                        nc.scalar.activation(col_b[:, :], col_a[:, :], ACT.Sqrt).then_inc(norm_root, 1)
                    if is_at(q, NB + 1) and c == 5:
                        take_row(1)
                    if is_at(q, 2 * NB + 1) and c == 3:
                        take_row(2)

            blocks(act, one)

        @block.vector
        def _(dve):
            def lo_of(dest, value, high, relu=False):
                if relu:
                    return nc.vector.scalar_tensor_tensor(out=dest, in0=value, scalar=0.0, in1=high.bitcast(f32),
                                                          op0=ALU.max, op1=ALU.subtract)
                return nc.vector.tensor_tensor(dest, value, high.bitcast(f32), ALU.subtract)

            def split_w(n):
                dve.wait_ge(w_hi_ready, n + 1)
                lo_of(w_lo[:, W_ORDER[n][1], :, :], w_raw[n], w_hi[:, W_ORDER[n][1], :, :]).then_inc(w_lo_ready, 1)

            def ln_sums(sources, at=0):
                for t, source in enumerate(sources):
                    ins = nc.vector.bn_stats(stats[:, at + t, :], source)
                return ins

            def ln_stats(sums, n, width):
                step = (n - 1) * LN_STEPS
                sums.then_inc(ln_step, 1)
                dve.wait_ge(ln_step, step + 1)
                dve.sem_inc(stats_seen, 1)
                for t in range(width):
                    ins = nc.vector.bn_aggr(mv[:, t, :], stats[:, t, :])
                ins.then_inc(ln_step, 1)
                dve.wait_ge(ln_step, step + 2)
                nc.vector.tensor_scalar(var[:, 0:width], mv[:, 0:width, 1], LN_EPS, None, ALU.add
                                        ).then_inc(var_ready, 1)
                nc.vector.tensor_scalar(nmean2[:, 0:width], mv[:, 0:width, 0], -2.0, None, ALU.mult
                                        ).then_inc(ln_step, 1)

            def ln_rstd(n, width):
                step = (n - 1) * LN_STEPS
                part = slice(0, width)
                dve.wait_ge(root_ready, n)
                nc.vector.reciprocal(quot[:, part], root[:, part]).then_inc(ln_step, 1)
                dve.wait_ge(ln_step, step + 4)
                nc.vector.tensor_tensor(quot[:, part], quot[:, part], var[:, part], ALU.mult).then_inc(ln_step, 1)
                dve.wait_ge(ln_step, step + 5)
                nc.vector.tensor_tensor(quot[:, part], quot[:, part], root[:, part], ALU.add).then_inc(ln_step, 1)
                dve.wait_ge(ln_step, step + 6)
                nc.vector.reciprocal(quot[:, part], quot[:, part]).then_inc(quot_ready, 1)
                dve.wait_ge(quot_ready, n)
                nc.vector.tensor_scalar(rstd[:, part], quot[:, part], 2.0, None, ALU.mult)
                nc.vector.tensor_tensor(shift[:, part], quot[:, part], nmean2[:, part], ALU.mult
                                        ).then_inc(rstd_ready, 1)

            def head_sums(b):
                return ln_sums([x_all[:, b, t, :] for t in range(IT)], b % 2 * IT)

            def head_h(b):
                dve.wait_ge(h_hi_ready, b + 1)
                lo_of(lo[:, b % 2, :].rearrange("p (k n) -> p k n", k=K), turned_of[b % 2],
                      hi[:, b % 2, :].rearrange("p (k n) -> p k n", k=K)).then_inc(h_lo_ready, 1)

            def head_g(b):
                dve.wait_ge(g_hi_ready, b + 1)
                lo_of(g_lo[0][:, tiles(b), :], made_of[b % 2], g_hi[0][:, tiles(b), :]).then_inc(g_lo_ready, 1)

            dve.wait_ge(x_loaded[0], 16)
            head_sums(0)
            ln_stats(head_sums(1), 1, 2 * IT)
            ln_rstd(1, 2 * IT)
            for n in range(3):
                split_w(n)
            for i in range(LN_HEAD):
                more = i + 1 < LN_HEAD
                if more:
                    dve.wait_ge(x_loaded[i + 1], 16)
                    dve.wait_ge(normed, 2 * i + 2)
                    head_sums(2 * i + 2)
                    ln_stats(head_sums(2 * i + 3), i + 2, 2 * IT)
                head_h(2 * i)
                head_h(2 * i + 1)
                if more:
                    ln_rstd(i + 2, 2 * IT)
                head_g(2 * i)
                head_g(2 * i + 1)
            split_w(3)

            def sum_chunk(q, layer, c):
                chunk = raw_at(layer, c)
                if not (is_first(q) and c == 0):
                    dve.wait_ge(acc_step, q * NC + c)
                dest = acc[:, :]
                if c == NC - 1:
                    dest = acc_end[layer]
                    if not is_first(q):
                        dve.wait_ge(cols_done, q)
                    if is_at(q, NB):
                        dve.wait_ge(h_stored, 16 * NB)
                if layer == GRAPH_1 and c == 0:
                    ins = nc.vector.tensor_scalar(dest, chunk, 0.0, None, ALU.is_gt)
                elif layer == GRAPH_1:
                    ins = nc.vector.scalar_tensor_tensor(out=dest, in0=chunk, scalar=0.0, in1=acc[:, :],
                                                         op0=ALU.is_gt, op1=ALU.add)
                elif c == 0:
                    ins = nc.vector.tensor_copy(dest, chunk)
                else:
                    ins = nc.vector.tensor_tensor(dest, acc[:, :], chunk, ALU.add)
                ins.then_inc(acc_step, 1)

            def fold(q, was):
                dve.wait_ge(acc_step, q * NC)
                nc.vector.tensor_tensor(folded[was], acc_end[was][:, 0:BW], acc_end[was][:, BW:CW],
                                        ALU.add).then_inc(fold_ready, 1)

            def split_chunk(q, layer, c):
                if not (is_first(q) and c < LO_RING):
                    dve.wait_ge(chunk_done, lo_free(q, layer, c))
                dve.wait_ge(hi_ready, splits(q, layer, c + 1))
                lo_of(lo_at(q, layer, c), raw_at(layer, c),
                      hi[:, slot(q, layer, c, HI_RING), :]).then_inc(lo_ready, 1)

            def incidence(q, c, half):
                scale = rn_row[:, half, :].rearrange("p (a n) -> p a n", a=1).broadcast_to([P, CT, BW])
                if is_at(q, 2 * NB) and c == 0:
                    dve.wait_ge(acc_step, q * NC)
                elif is_at(q, 2 * NB) and c == 1:
                    dve.wait_ge(chunk_done, q * NC)
                else:
                    dve.wait_ge(inc_ready, (q - 2 * NB) * NC + (c - 1))
                nc.vector.scalar_tensor_tensor(
                    out=(acc, step_more)[c % 2][:, :].rearrange("p (t n) -> p t n", t=CT),
                    in0=raw_at(HYPER, c).rearrange("p (t n) -> p t n", t=CT), scalar=0.0, in1=scale,
                    op0=ALU.is_gt, op1=ALU.mult).then_inc(acc_step, 1)

            def add_incidence(q, c):
                dve.wait_ge(acc_step, q * NC + (c + 1))
                nc.vector.tensor_tensor(raw_at(HYPER, c), raw_at(HYPER, c), (acc, step_more)[c % 2][:, :],
                                        ALU.add).then_inc(inc_ready, 1)

            def behind(q, layer, c):
                old_q, old_layer, old_c = chunk_before(q, layer, c, 1)
                if old_layer == HYPER:
                    add_incidence(old_q, old_c)
                old_q, old_layer, old_c = chunk_before(q, layer, c, 2)
                if old_layer == HYPER and not whole(old_q, old_layer, old_c):
                    split_chunk(old_q, old_layer, old_c)

            def after_graph_1(c, q, b, half):
                if c == TAKE:
                    dve.wait_ge(h_hi_ready, q + NB)
                    lo_of(h_new[:, LO, :, :], main[:, half, :, :], h_new[:, HI, :, :],
                          relu=True).then_inc(h_lo_ready, 1)
                if c == SPLIT_MADE:
                    dve.wait_ge(g_hi_ready, q + NB)
                    lo_of(g_lo[1][:, tiles(b), :], made[:, :, :], g_hi[1][:, tiles(b), :]).then_inc(g_lo_ready, 1)

            def after_graph_2(c, q, b, half):
                if c == TAKE:
                    dve.wait_ge(chunk_done, q * NC)
                    dve.wait_ge(xblk_loaded, (q - NB) * 16)
                    nc.vector.scalar_tensor_tensor(out=xblk[:, :, :], in0=main[:, half, :, :], scalar=0.0,
                                                   in1=xblk[:, :, :], op0=ALU.max, op1=ALU.add
                                                   ).then_inc(xblk_ready, 1)
                if c == STATS:
                    dve.wait_ge(made_done, q + NB)
                    ln_stats(ln_sums([made[:, t, :] for t in range(IT)]), q - NB + LN_HEAD, IT)
                if c == RSTD:
                    ln_rstd(q - NB + LN_HEAD, IT)
                if c == SPLIT_NORM:
                    dve.wait_ge(g_hi_ready, q + NB)
                    lo_of(g_lo[0][:, tiles(b), :], nat[:, :, :], g_hi[0][:, tiles(b), :]).then_inc(g_lo_ready, 1)

            def after_hyper(q, half):
                dve.wait_ge(chunk_done, q * NC)
                dve.wait_ge(rd_loaded, (q - 2 * NB) * 16)
                scale = rd_row[:, 0:BW].rearrange("p (a n) -> p a n", a=1).broadcast_to([P, K, BW])
                result = nat[:, :, :].rearrange("p t d -> p (t d)").rearrange("p (k n) -> p k n", k=K)
                nc.vector.tensor_tensor(result, main[:, half, :, :], scale, ALU.mult).then_inc(product, 1)
                dve.wait_ge(product, q - 2 * NB)
                dve.wait_ge(xblk_loaded, (q - NB) * 16)
                nc.vector.tensor_tensor(xblk[:, :, :], result, xblk[:, :, :], ALU.add).then_inc(xblk_ready, 1)

            def norms():
                dve.wait_ge(norm_root, 1)
                nc.vector.reciprocal(rn[:, :], col_b[:, :]).then_inc(cols_step, 1)
                dve.wait_ge(cols_step, 2)
                nc.vector.tensor_tensor(rn[:, :], rn[:, :], col_a[:, :], ALU.mult).then_inc(cols_step, 1)
                dve.wait_ge(cols_step, 3)
                nc.vector.tensor_tensor(rn[:, :], rn[:, :], col_b[:, :], ALU.add).then_inc(cols_step, 1)
                dve.wait_ge(cols_step, 4)
                nc.vector.tensor_scalar(rn[:, :], rn[:, :], 0.5, NORM_EPS, ALU.mult, ALU.max).then_inc(cols_step, 1)
                dve.wait_ge(cols_step, 5)
                nc.vector.reciprocal(rn[:, :], rn[:, :]).then_inc(cols_step, 1)

            def degrees():
                dve.wait_ge(cols_taken, 2 * NB)
                nc.vector.tensor_tensor(col_a[:, :], cnt[:, :], rn[:, :], ALU.mult).then_inc(cols_step, 1)
                dve.wait_ge(cols_step, 7)
                nc.vector.tensor_tensor(col_a[:, :], col_a[:, :], rsum[:, :], ALU.add).then_inc(cols_step, 1)
                dve.wait_ge(cols_step, 8)
                nc.vector.reciprocal(rdeg[:, :], col_a[:, :]).then_inc(cols_step, 1)

            def one(q, layer, b, half):
                for c in range(NC):
                    wait_raw(dve, q, layer, c)
                    if layer == HYPER:
                        if c == 0:
                            loads = 1 if isinstance(b, int) else None
                            if loads:
                                dve.wait_ge(rn_loaded[half], 16)
                            else:
                                dve.wait_ge(rn_loaded[half], (b - half) * 8 + 16)
                        incidence(q, c, half)
                        behind(q, layer, c)
                    else:
                        sum_chunk(q, layer, c)
                        split_chunk(q, layer, c)
                    if not is_first(q):
                        was, last_b = before(q, layer, b)
                        if was == GRAPH_1:
                            after_graph_1(c, q, last_b, 1 - half)
                        if was == GRAPH_2:
                            after_graph_2(c, q, last_b, 1 - half)
                        if was != HYPER and c == FOLD:
                            fold(q, was)
                        if was == HYPER and c == FINISH:
                            after_hyper(q, 1 - half)
                    if is_at(q, NB) and c == NC - 2:
                        dve.wait_ge(cols_taken, NB)
                        nc.vector.tensor_scalar(col_a[:, :], cnt[:, :], NORM_EPS * NORM_EPS, None,
                                                ALU.max).then_inc(cols_step, 1)
                    if is_at(q, NB) and c == NC - 1:
                        norms()
                    if is_at(q, 2 * NB) and c == NC - 1:
                        degrees()

            blocks(dve, one)
            behind(3 * NB, HYPER, 0)
            after_hyper(3 * NB, 1)

        @block.tensor
        def _(pe):
            def three(dest, stationary, moving, start, stop):
                nc.tensor.matmul(dest, stationary[HI], moving[HI], start=start, stop=False)
                nc.tensor.matmul(dest, stationary[LO], moving[HI], start=False, stop=False)
                return nc.tensor.matmul(dest, stationary[HI], moving[LO], start=False, stop=stop)

            def times_wb(dest, h):
                for t in range(IT):
                    for k in range(K):
                        ins = three(dest[:, t, :], [part[:, k, t * P:(t + 1) * P] for part in h],
                                    (w_hi[:, WB, k, :], w_lo[:, WB, k, :]), k == 0, k == K - 1)
                ins.then_inc(made_done, 1)

            def head_turn(b):
                pe.wait_ge(normed, b + 1)
                for t in range(IT):
                    for k in range(K):
                        ins = nc.tensor.transpose(turned_of[b % 2][:, k, t * P:(t + 1) * P],
                                                  x_all[:, b, t, k * P:(k + 1) * P], ident[:, :])
                ins.then_inc(turned_done, 1)

            def head_times(b):
                pe.wait_ge(h_lo_ready, b + 1)
                if b >= 2:
                    pe.wait_ge(g_lo_ready, b - 1)
                times_wb(made_of[b % 2], [part[:, b % 2, :].rearrange("p (k n) -> p k n", k=K)
                                          for part in (hi, lo)])

            pe.wait_ge(const_step, 3)
            pe.wait_ge(w_lo_ready, 1)
            for i in range(LN_HEAD):
                head_turn(2 * i)
                head_turn(2 * i + 1)
                head_times(2 * i)
                head_times(2 * i + 1)
            pe.wait_ge(w_lo_ready, 3)
            pe.wait_ge(ones_ready, 1)

            def times_wa(q, layer, half, k):
                pe.wait_ge(h_loaded, q * (16 * K) + 16 * (k + 1))
                place = (WA_1, WA_2)[layer]
                for f in range(K):
                    weight = [m[:, place, k, f * P:(f + 1) * P] for m in (w_hi, w_lo)]
                    ins = three(main[:, half, f, :], weight, [h_old[:, s, :] for s in (HI, LO)], False, False)
                ins.then_inc(h_used, 1)

            def made_free(number):
                pe.wait_ge(g_hi_ready, number - 1)
                pe.wait_ge(g_lo_ready, number - 1)

            def sum_columns(q, was):
                pe.wait_ge(fold_ready, q)
                if not is_at(q, 1):
                    pe.wait_ge(cols_taken, q - 1)
                if is_at(q, NB + 1):
                    pe.wait_ge(row_ready, 1)
                for t in range(IT):
                    ins = nc.tensor.matmul(turned[:, 0, 2 * t:2 * t + 2], folded[was][:, t * P:(t + 1) * P],
                                           (ones_r, ones)[was][:, :], start=True, stop=True)
                ins.then_inc(cols_done, 1)

            def turn_cols(source, step, number):
                pe.wait_ge(cols_step, step)
                pe.wait_ge(cols_taken, number * NB)
                nc.tensor.transpose(turned[0:N // P, 0, 0:P], source[:, :], ident[:, :]).then_inc(row_turned, 1)

            def after_graph_1(c, q):
                if c == MAKE:
                    if is_at(q, 1):
                        pe.wait_ge(w_lo_ready, 4)
                    pe.wait_ge(h_lo_ready, q + NB)
                    made_free(q + NB)
                    times_wb(made, [h_new[:, s, :, :] for s in (HI, LO)])

            def after_graph_2(c, q):
                if c == MAKE:
                    pe.wait_ge(xblk_ready, q - NB)
                    made_free(q + NB)
                    for t in range(IT):
                        for k in range(K):
                            ins = nc.tensor.transpose(made[:, t, k * P:(k + 1) * P],
                                                      xblk[:, k, t * P:(t + 1) * P], ident[:, :])
                    ins.then_inc(made_done, 1)

            def one(q, layer, b, half):
                if layer == GRAPH_1 and is_first(q):
                    pe.wait_ge(g_lo_ready, NB)
                elif not (isinstance(q, int) and q < 2):
                    if layer == GRAPH_1 or is_at(q, NB) or is_at(q, NB + 1):
                        pe.wait_ge(h_lo_ready, q + (NB - 1))
                    else:
                        pe.wait_ge(xblk_ready, q - (NB + 1))
                if isinstance(b, int) and b == 0 and layer:
                    pe.wait_ge(g_lo_ready, (layer + 1) * NB - 1)
                at = layer % 2
                for c in range(NC):
                    if isinstance(b, int) and b == 0 and layer and c * CT == (NB - 1) * IT:
                        pe.wait_ge(g_lo_ready, (layer + 1) * NB)
                    ends = c == NC - 1
                    if whole(q, layer, c):
                        if is_at(q, 2 * NB) or is_at(q, 2 * NB + 1):
                            pe.wait_ge(g_loaded[c * CT // IT], 16)
                        pe.wait_ge(inc_ready, (q - 2 * NB) * NC + (c + 1))
                        for s in range(CT):
                            for f in range(K):
                                ins = nc.tensor.matmul(main[:, half, f, :],
                                                       g_whole[:, c * CT + s, f * P:(f + 1) * P],
                                                       raw_at(layer, c)[:, s * BW:(s + 1) * BW],
                                                       start=c + s == 0, stop=ends and s == CT - 1)
                    else:
                        pe.wait_ge(hi_ready, splits(q, layer, c + 1))
                        pe.wait_ge(lo_ready, splits(q, layer, c + 1))
                        parts = (hi[:, slot(q, layer, c, HI_RING), :], lo_at(q, layer, c))
                        for s in range(CT):
                            for f in range(K):
                                g = [m[at][:, c * CT + s, f * P:(f + 1) * P] for m in (g_hi, g_lo)]
                                ins = three(main[:, half, f, :], g,
                                            [part[:, s * BW:(s + 1) * BW] for part in parts],
                                            c + s == 0, ends and s == CT - 1)
                    ins.then_inc(chunk_done, 1)
                    if layer != HYPER and c in WA_AT:
                        times_wa(q, layer, half, WA_AT.index(c))
                    if not is_first(q):
                        was, last_b = before(q, layer, b)
                        if was == GRAPH_1:
                            after_graph_1(c, q)
                        if was == GRAPH_2:
                            after_graph_2(c, q)
                        if was != HYPER and c == COUNT:
                            sum_columns(q, was)
                    if is_at(q, NB + 1) and c == 1:
                        turn_cols(rn, 6, 1)
                    if is_at(q, 2 * NB + 1) and c == 1:
                        turn_cols(rdeg, 9, 2)

            blocks(pe, one)


def kernel(x, adj, L0_gnn_W1, L0_gnn_W2):
    import numpy as np
    import concourse.bacc as bacc
    from concourse.bass_utils import run_bass_kernel_spmd

    x, adj, w1, w2 = (np.asarray(a) for a in (x, adj, L0_gnn_W1, L0_gnn_W2))
    f32 = mybir.dt.float32
    arrays = {
        "adj_t": adj.reshape(NB, BW, NC, CT, P).transpose(0, 2, 4, 3, 1).reshape(NB, NC, P, CW),
        "x_rows": x.reshape(NB, IT, P, D).transpose(0, 2, 1, 3),
        "x_cols": x.reshape(NB, BW, K, P).transpose(0, 3, 2, 1).reshape(NB, P, K * BW),
        "w": np.stack([w1, w2]).reshape(4, K, P, D).transpose(0, 2, 1, 3),
    }
    arrays = {name: np.ascontiguousarray(a) for name, a in arrays.items()}
    nc = bacc.Bacc("TRN2", target_bir_lowering=False, num_devices=1)
    ins = [nc.dram_tensor(name, a.shape, f32, kind="ExternalInput").ap() for name, a in arrays.items()]
    out = nc.dram_tensor("out", (NB, P, K * BW), f32, kind="ExternalOutput").ap()
    h_mem = nc.dram_tensor("h_mem", (2, NB, K, P, 2, BW), f32, kind="Internal").ap()
    g_mem = nc.dram_tensor("g_mem", (NB, P, IT, D), f32, kind="Internal").ap()
    x1_mem = nc.dram_tensor("x1_mem", (NB, P, K * BW), f32, kind="Internal").ap()
    rn_mem = nc.dram_tensor("rn_mem", (NB, BW), f32, kind="Internal").ap()
    rd_mem = nc.dram_tensor("rd_mem", (NB, BW), f32, kind="Internal").ap()
    gnn_kernel(nc, *ins, out, h_mem, g_mem, x1_mem, rn_mem, rd_mem)
    result = run_bass_kernel_spmd(nc, [arrays], core_ids=[0]).results[0]["out"]
    return np.ascontiguousarray(result.reshape(NB, P, K, BW).transpose(0, 3, 2, 1)).reshape(N, D)
```

```python
import concourse.bass as bass
from concourse import mybir
from contextlib import ExitStack

P = 128
N = 4096
D = 256
K = D // P
BW = 512
NB = N // BW
IT = BW // P
CT = 2
CW = CT * BW
NC = N // (P * CT)
RING, RING_MORE = 4, 4
HI_RING = 4
LO_RING, LO_MORE = 2, 2
LN_EPS = 1e-5
NORM_EPS = 1e-12
GRAPH_1, GRAPH_2, HYPER = range(3)
WA_1, WB, WA_2 = range(3)
HI, LO = range(2)

WHOLE = range(1, NC, 4)
WHOLE_FIRST = range(3 * NC // 8, NC - NC // NB)
ADDED = WHOLE
ADD_RING = 4
PRE = (3, 11)
PRE_FROM = 2

TAKE = 1
MAKE = 3
SPLIT_MADE, SPLIT_MADE_HI = 5, 7
STATS, ROOT, RSTD = 5, 7, 7
NORM, SPLIT_NORM = 9, 9
TAKE_HYPER = 2
STATS_HYPER, ROOT_HYPER, RSTD_HYPER, NORM_HYPER, SPLIT_NORM_HYPER = 7, 7, 9, 9, 12
WA_AT = (4, 9)
FOLD = 2
COUNT, COUNT_TAKE = 10, 14
SPREAD, FETCH, STORE_OUT = 1, 5, 13
FINISH = 9
LN_STEPS = 6
LN_HEAD = NB // 2
HEAD_RING = 4
HEAD_CHUNKS = NC // NB


def gnn_kernel(nc, adj_t, x_rows, x_cols, w, out, h_mem, g_mem, x1_mem, rn_mem, rd_mem, inc_mem):
    f32, f32r = mybir.dt.float32, mybir.dt.float32r
    ALU, ACT = mybir.AluOpType, mybir.ActivationFunctionType

    with ExitStack() as ctx:
        def sb(name, shape, dt=f32, where=ctx):
            return where.enter_context(nc.sbuf_tensor(name, shape, dt))

        def sem(name):
            return ctx.enter_context(nc.semaphore(name))

        with ExitStack() as graph_only:
            g_lo_1 = sb("g_lo1", [P, N // P, D], f32r, graph_only)
        with ExitStack() as head_only:
            h_head = sb("h_head", [P, 2, HEAD_RING, CW], f32r, head_only)
        raw_more = sb("raw_more", [P, RING_MORE, CW])
        lo_more = sb("lo_more", [P, LO_MORE, CW], f32r)
        step_more = sb("step_more", [P, CW])
        rd_row = sb("rd_row", [P, CW])
        g_lo = [sb("g_lo0", [P, N // P, D], f32r), g_lo_1]
        with ExitStack() as head_only:
            x_all = sb("x_all", [P, NB, IT, D], f32, head_only)
        with ExitStack() as graph_only:
            g_hi_1 = sb("g_hi1", [P, N // P, D], f32r, graph_only)
        g_whole = sb("g_whole", [P, N // P, D])
        g_hi = [sb("g_hi0", [P, N // P, D], f32r), g_hi_1]
        raw = sb("raw", [P, RING, CW])
        hi = sb("hi", [P, HI_RING, CW], f32r)
        lo = sb("lo", [P, LO_RING, CW], f32r)
        with ExitStack() as graph_only:
            w_hi = sb("w_hi", [P, 3, K, D], f32r, graph_only)
            w_lo = sb("w_lo", [P, 3, K, D], f32r, graph_only)
            h_old = sb("h_old", [P, 2, BW], f32r, graph_only)
        step_added = sb("step_added", [P, ADD_RING, CW])
        xblk = sb("xblk", [P, K, BW])
        nat = sb("nat", [P, IT, D])
        acc = sb("acc", [P, CW])
        ident = sb("ident", [P, P])
        ones = sb("ones", [P, 2])
        ones_r = sb("ones_r", [P, 2], f32r)
        stats = sb("stats", [P, 2 * IT, 6])
        mv = sb("mv", [P, 2 * IT, 2])
        nmean2 = sb("nmean2", [P, 2 * IT])
        var = sb("var", [P, 2 * IT])
        root = sb("root", [P, 2 * IT])
        quot = sb("quot", [P, 2 * IT])
        rstd = sb("rstd", [P, 2 * IT])
        shift = sb("shift", [P, 2 * IT])
        cnt = sb("cnt", [P, N // P])
        rsum = sb("rsum", [P, N // P])
        col_a = sb("col_a", [P, N // P])
        col_b = sb("col_b", [P, N // P])
        rn = sb("rn", [P, N // P])
        rdeg = sb("rdeg", [P, N // P])
        with ExitStack() as early:
            h_new = sb("h_new", [P, 2, K, BW], f32r, early)
            count_fold = sb("count_fold", [P, BW], f32r, early)
        rn_row = sb("rn_row", [P, 2, BW])
        sum_fold = sb("sum_fold", [P, BW])
        pre = sb("pre", [P, CW])
        row = pre[0:N // P, 0:P]
        acc_end = [nat[:, :, :].rearrange("p t d -> p (t d)"), acc[:, :]]
        folded = [count_fold[:, :], sum_fold[:, :]]

        main = ctx.enter_context(nc.psum_tensor("main", [P, 2, K, BW], f32))
        turned = ctx.enter_context(nc.psum_tensor("turned", [P, K, BW], f32))
        made = ctx.enter_context(nc.psum_tensor("made", [P, IT, D], f32))

        made_of = [made[:, :, :], main[:, 1, :, :].rearrange("p k (t d) -> p (k t) d", d=D)]

        raw_full = [sem(f"raw_full{r}") for r in range(RING + RING_MORE)]
        inc_ready = sem("inc_ready")
        pre_step = sem("pre_step")
        pre_ready = sem("pre_ready")
        pre_stored = sem("pre_stored")
        inc_added = [sem(f"inc_added{r}") for r in range(ADD_RING)]
        hi_ready = sem("hi_ready")
        lo_ready = sem("lo_ready")
        acc_step = sem("acc_step")
        fold_ready = sem("fold_ready")
        chunk_done = sem("chunk_done")
        group_done = sem("group_done")
        h_hi_ready = sem("h_hi_ready")
        h_lo_ready = sem("h_lo_ready")
        h_stored = sem("h_stored")
        h_loaded = sem("h_loaded")
        h_used = sem("h_used")
        turned_done = sem("turned_done")
        head_stored = [sem(f"head_stored{s}") for s in range(HEAD_RING)]
        made_done = sem("made_done")
        g_hi_ready = sem("g_hi_ready")
        g_lo_ready = sem("g_lo_ready")
        x_loaded = [sem(f"x_loaded{i}") for i in range(LN_HEAD)]
        x_first = sem("x_first")
        normed = sem("normed")
        g_stored = sem("g_stored")
        g_loaded = [sem(f"g_loaded{b}") for b in range(NB)]
        xblk_loaded = sem("xblk_loaded")
        xblk_ready = sem("xblk_ready")
        xblk_stored = sem("xblk_stored")
        out_stored = sem("out_stored")
        last_stored = sem("last_stored")
        ln_step = sem("ln_step")
        quot_ready = sem("quot_ready")
        var_ready = sem("var_ready")
        root_ready = sem("root_ready")
        rstd_ready = sem("rstd_ready")
        w_loaded = [sem(f"w_loaded{n}") for n in range(4)]
        w_hi_ready = sem("w_hi_ready")
        w_lo_ready = sem("w_lo_ready")
        cols_done = sem("cols_done")
        cols_taken = sem("cols_taken")
        cols_step = sem("cols_step")
        norm_root = sem("norm_root")
        row_turned = sem("row_turned")
        row_ready = sem("row_ready")
        row_stored = sem("row_stored")
        rn_loaded = [sem(f"rn_loaded{s}") for s in range(2)]
        rd_loaded = sem("rd_loaded")
        product = sem("product")
        const_step = sem("const_step")
        ones_ready = sem("ones_ready")
        stats_seen = sem("stats_seen")
        block_seen = sem("block_seen")
        pre_seen = sem("pre_seen")

        block = ctx.enter_context(nc.Block())

        def blocks(eng, one):
            for layer in (GRAPH_1, GRAPH_2, HYPER):
                for b in range(2):
                    if layer or b:
                        one(NB * layer + b, layer, b, b)
                with eng.Fori(1, NB // 2) as pair:
                    for half in range(2):
                        b = 2 * pair + half
                        one(b + NB * layer, layer, b, half)

        def head_chunks(b):
            return range(b * HEAD_CHUNKS, (b + 1) * HEAD_CHUNKS) if b >= 0 else range(0)

        def head_part(part, b):
            return h_head[:, part, b % HEAD_RING, :]

        def is_first(q):
            return isinstance(q, int) and q == 0

        def is_at(q, number):
            return isinstance(q, int) and q == number

        def before(q, layer, b):
            if isinstance(b, int) and b == 0:
                return layer - 1, NB - 1
            return layer, b - 1

        def tiles(b):
            return bass.ds(b * IT, IT)

        W_ORDER = [(1, WB), (0, WA_1), (2, WA_2), (3, WB)]
        w_raw = [xblk[:, n, :].rearrange("p (k d) -> p k d", k=K) for n in range(2)]
        w_raw += [nat[:, 2 * n:2 * n + 2, :] for n in range(2)]

        def whole(q, layer, c):
            return layer == HYPER and c in (WHOLE_FIRST if is_at(q, 2 * NB) else WHOLE)

        def split_list(q, layer):
            return [c for c in range(NC) if not whole(q, layer, c)]

        def splits(q, layer, c):
            here = sum(not whole(q, layer, a) for a in range(c))
            if layer != HYPER or is_at(q, 2 * NB):
                return q * NC + here
            return (q - (2 * NB + 1)) * (NC - len(WHOLE)) + (2 * NB + 1) * NC - len(WHOLE_FIRST) + here

        def chunk_before(q, layer, c, back):
            if c >= back:
                return q, layer, c - back
            return q - 1, before(q, layer, b_of(q, layer))[0], c - back + NC

        def b_of(q, layer):
            return q - NB * layer

        def ring_of(layer):
            return RING + RING_MORE if layer == HYPER else RING

        def raw_at(layer, c):
            r = c % ring_of(layer)
            return raw[:, r, :] if r < RING else raw_more[:, r - RING, :]

        def wait_raw(eng, q, layer, c):
            ring = ring_of(layer)
            loads = 16 * (c // ring + 1)
            if layer != HYPER:
                eng.wait_ge(raw_full[c % ring], q * (16 * NC // ring) + loads)
            else:
                if c % ring < RING:
                    loads += 2 * NB * (16 * NC // RING)
                eng.wait_ge(raw_full[c % ring], (q - 2 * NB) * (16 * NC // ring) + loads)

        def lo_ring(layer):
            return LO_RING + LO_MORE if layer == HYPER else LO_RING

        def lo_at(q, layer, c):
            r = slot(q, layer, c, lo_ring(layer))
            return lo[:, r, :] if r < LO_RING else lo_more[:, r - LO_RING, :]

        def lo_free(q, layer, c):
            n = split_list(q, layer).index(c)
            if is_at(q, 2 * NB) and n < LO_RING:
                return last_of_slot(q, layer, c, LO_RING)
            if is_at(q, 2 * NB) and n < LO_RING + LO_MORE:
                return q * NC
            return last_of_slot(q, layer, c, lo_ring(layer))

        def made_before(q, c):
            return c in PRE and not any(is_at(q, 2 * NB + b) for b in range(PRE_FROM))

        def by_dma(q, c):
            return not is_at(q, 2 * NB) and c in ADDED

        def count(q, here, first, second, others):
            if is_at(q, 2 * NB):
                return here
            if is_at(q, 2 * NB + 1):
                return first + here
            return (q - (2 * NB + 2)) * others + (first + second + here)

        def steps(q, c):
            here = sum(not made_before(q, a) for a in range(c))
            return count(q, here, NC, NC, NC - len(PRE)) + 2 * NB * NC

        def sums(q, c):
            here = sum(not by_dma(q, a) and not made_before(q, a) for a in range(c))
            return count(q, here, NC, NC - len(ADDED), NC - len(ADDED) - len(PRE))

        def added(q, c):
            return (q - (2 * NB + 1)) * (16 * len(ADDED) // ADD_RING) + 16 * (ADDED.index(c) // ADD_RING + 1)

        def pre_number(b, c):
            return (b - PRE_FROM) * len(PRE) + PRE.index(c)

        def add_slot(c):
            return ADDED.index(c) % ADD_RING

        def wait_inc(eng, q, c):
            if made_before(q, c):
                wait_raw(eng, q, HYPER, c)
            elif by_dma(q, c):
                eng.wait_ge(inc_added[add_slot(c)], added(q, c))
            else:
                eng.wait_ge(inc_ready, sums(q, c + 1))

        def last_of_slot(q, layer, c, ring):
            n = split_list(q, layer).index(c) - ring
            if n >= 0:
                return q * NC + (split_list(q, layer)[n] + 1)
            was = before(q, layer, b_of(q, layer))[0]
            return (q - 1) * NC + (split_list(q - 1, was)[n] + 1)

        def slot(q, layer, c, ring):
            return split_list(q, layer).index(c) % ring

        @block.sync
        def _(sp):
            def load_chunk(layer, b, c):
                source = adj_t[b, c, :, :]
                if layer == HYPER and made_before(b + 2 * NB, c):
                    sp.sem_inc(pre_seen, 1)
                    sp.wait_ge(pre_stored, pre_number(b, c) * 16 + 32)
                    sp.sem_inc(pre_seen, 1)
                    source = inc_mem[b, PRE.index(c), :, :]
                sp.dma_start(raw_at(layer, c), source).then_inc(raw_full[c % ring_of(layer)], 16)

            sp.sem_inc(pre_stored, 16)
            for b in range(2):
                sp.dma_start(x_all[:, b, :, :], x_rows[b, :, :, :]).then_inc((x_first, x_loaded[0])[b], 16)
            for i in range(1, LN_HEAD):
                sp.dma_start(x_all[:, 2 * i:2 * i + 2, :, :], x_rows[2 * i:2 * i + 2, :, :, :].rearrange(
                    "b p t d -> p b t d")).then_inc(x_loaded[i], 16)
            for c in range(RING):
                load_chunk(GRAPH_1, 0, c)

            def load(q, layer, b, c):
                if is_first(q) and c < RING:
                    return
                new = is_at(q, 2 * NB) and RING <= c < RING + RING_MORE
                back = RING if is_at(q, 2 * NB) and c < RING else ring_of(layer)
                old_q, old_layer, old_c = chunk_before(q, layer, c, back)
                if new:
                    sp.wait_ge(chunk_done, q * NC)
                elif whole(old_q, old_layer, old_c):
                    sp.wait_ge(chunk_done, old_q * NC + (old_c + 1))
                else:
                    sp.wait_ge(hi_ready, splits(old_q, old_layer, old_c + 1))
                    sp.wait_ge(lo_ready, splits(old_q, old_layer, old_c + 1))
                if layer == GRAPH_2 and made_before(q + NB, old_c):
                    sp.sem_inc(pre_seen, 1)
                    sp.wait_ge(pre_ready, pre_number(b, old_c) + 1)
                    sp.sem_inc(pre_seen, 1)
                    sp.dma_start(inc_mem[b, PRE.index(old_c), :, :], pre[:, :]).then_inc(pre_stored, 16)
                load_chunk(layer, b, c)

            def store_head(b):
                for part, ready in ((HI, h_hi_ready), (LO, h_lo_ready)):
                    sp.wait_ge(ready, b + 1)
                    sp.dma_start(h_mem[GRAPH_1, b, :, :, part, :].rearrange("k p n -> p k n"),
                                 head_part(part, b).bitcast(f32).rearrange("p (k n) -> p k n", k=K)
                                 ).then_inc(head_stored[b % HEAD_RING], 16)

            for b in range(NB):
                store_head(b)
                for c in head_chunks(b - 1):
                    if c + RING < NC:
                        load(0, GRAPH_1, 0, c + RING)

            def one(q, layer, b, half):
                for c in range(NC):
                    load(q, layer, b, c)

            blocks(sp, one)
            for k in range(K):
                sp.wait_ge(xblk_ready, 2 * NB + k)
                sp.dma_start(out[NB - 1, :, k * BW:(k + 1) * BW], xblk[:, k, :]).then_inc(last_stored, 16)
            sp.wait_ge(last_stored, 16 * K)

        @block.gpsimd
        def _(pool):
            for n in range(4):
                pool.dma_start(w_raw[n], w[W_ORDER[n][0], :, :, :]).then_inc(w_loaded[n], 16)
            nc.gpsimd.memset(ident[:, :], 0.0).then_inc(const_step, 1)
            nc.gpsimd.memset(ones[:, :], 1.0).then_inc(const_step, 1)
            pool.wait_ge(const_step, 2)
            nc.gpsimd.affine_select(out=ident[:, :], in_=ident[:, :], compare_op=ALU.not_equal, fill=1.0,
                                    base=0, pattern=[[-1, P]], channel_multiplier=1).then_inc(const_step, 1)

            def load_h(q, layer, b, k):
                if not (is_first(q) and k == 0):
                    pool.wait_ge(h_used, q * K + k)
                pool.dma_start(h_old[:, :, :].bitcast(f32), h_mem[layer, b, k, :, :, :]).then_inc(h_loaded, 16)

            def store_h(q):
                pool.wait_ge(h_hi_ready, q + NB)
                pool.wait_ge(h_lo_ready, q + NB)
                pool.dma_start(h_mem[GRAPH_2, q - 1, :, :, :, :].rearrange("k p s n -> p s k n"),
                               h_new[:, :, :, :].bitcast(f32)).then_inc(h_stored, 16)
                pool.wait_ge(h_stored, q * 16)

            def load_xblk(source):
                pool.dma_start(xblk[:, :, :].rearrange("p k n -> p (k n)"), source).then_inc(xblk_loaded, 16)

            def load_x_cols(b):
                if not is_at(b, 0):
                    pool.wait_ge(made_done, b + 2 * NB)
                load_xblk(x_cols[b, :, :])

            def store_x1(b):
                pool.wait_ge(xblk_ready, b + 1)
                pool.sem_inc(block_seen, 1)
                pool.dma_start(x1_mem[b, :, :], xblk[:, :, :].rearrange("p k n -> p (k n)")
                               ).then_inc(xblk_stored, 16)
                pool.wait_ge(xblk_stored, (b + 1) * 16)

            def store_g(b):
                pool.wait_ge(normed, b + (NB + 1))
                pool.sem_inc(block_seen, 1)
                pool.dma_start(g_mem[b, :, :, :], nat[:, :, :]).then_inc(g_stored, 16)
                pool.wait_ge(g_stored, (b + 1) * 16)

            def spread(dest, mem, b, done):
                pool.dma_start(dest, mem[bass.ds(b, 1), :].partition_broadcast(P)).then_inc(done, 16)

            def store_row(number, mem):
                pool.wait_ge(row_ready, number)
                pool.dma_start(mem.rearrange("b (t p) -> (b t) p", p=P), row).then_inc(row_stored, 16)
                pool.wait_ge(row_stored, number * 16)

            pool.wait_ge(head_stored[0], 32)
            load_h(0, GRAPH_1, 0, 0)
            load_h(0, GRAPH_1, 0, 1)
            for ring in head_stored:
                pool.wait_ge(ring, 32 * NB // HEAD_RING)
            load_h(1, GRAPH_1, 1, 0)
            with pool.Fori(1, NB - 1) as q:
                load_h(q, GRAPH_1, q, 1)
                store_h(q)
                load_h(q + 1, GRAPH_1, q + 1, 0)
            load_h(NB - 1, GRAPH_1, NB - 1, 1)
            store_h(NB - 1)
            load_h(NB, GRAPH_2, 0, 0)

            load_h(NB, GRAPH_2, 0, 1)
            load_x_cols(0)
            store_h(NB)
            load_h(NB + 1, GRAPH_2, 1, 0)
            load_h(NB + 1, GRAPH_2, 1, 1)
            store_x1(0)
            store_row(1, rn_mem)
            spread(rn_row[:, 0, :], rn_mem, PRE_FROM, rn_loaded[0])
            store_g(0)
            load_h(NB + 2, GRAPH_2, 2, 0)

            def second(b, half):
                load_x_cols(b - 1)
                load_h(b + NB, GRAPH_2, b, 1)
                store_x1(b - 1)
                store_g(b - 1)
                spread(rn_row[:, 1 - half, :], rn_mem, b + 1, rn_loaded[1 - half])
                load_h(b + (NB + 1), GRAPH_2, b + 1, 0)

            with pool.Fori(1, NB // 2 - 1) as pair:
                for half in range(2):
                    second(2 * pair + half, half)
            second(NB - 2, 0)
            load_x_cols(NB - 2)
            load_h(2 * NB - 1, GRAPH_2, NB - 1, 1)
            store_x1(NB - 2)
            store_g(NB - 2)
            spread(rn_row[:, 0, :], rn_mem, 0, rn_loaded[0])

            def load_g(b):
                pool.dma_start(g_whole[:, b * IT:(b + 1) * IT, :], g_mem[b, :, :, :]).then_inc(g_loaded[b], 16)

            load_x_cols(NB - 1)
            pool.wait_ge(chunk_done, 2 * NB * NC)
            for b in range(NB // 2 - 1, NB - 1):
                load_g(b)
            pool.wait_ge(pre_ready, (NB - PRE_FROM) * len(PRE))
            spread(rn_row[:, 1, :], rn_mem, 1, rn_loaded[1])
            store_x1(NB - 1)
            for b in range(NB // 2 - 1):
                load_g(b)
            store_g(NB - 1)
            load_g(NB - 1)

            def add_chunk(q, c):
                pool.wait_ge(acc_step, steps(q, c + 1))
                pool.sem_inc(block_seen, 1)
                pool.dma_start(raw_at(HYPER, c), step_added[:, add_slot(c), :], accum_op=ALU.add
                               ).then_inc(inc_added[add_slot(c)], 16)

            def fetch(b):
                load_xblk(x1_mem[b, :, :])
                spread(rd_row[:, 0:BW], rd_mem, b, rd_loaded)

            def store_out(b):
                pool.wait_ge(xblk_ready, b + (NB + 1))
                pool.sem_inc(block_seen, 1)
                pool.dma_start(out[b, :, :], xblk[:, :, :].rearrange("p k n -> p (k n)")
                               ).then_inc(out_stored, 16)
                pool.wait_ge(out_stored, b * 16 + 16)

            def last(b, half):
                q = b + 2 * NB
                for c in ADDED:
                    add_chunk(q, c)
                    if c == SPREAD and not is_at(b, NB - 1):
                        pool.wait_ge(acc_step, steps(q, 0))
                        spread(rn_row[:, 1 - half, :], rn_mem, b + 1, rn_loaded[1 - half])
                    if c == FETCH:
                        if is_at(b, 1):
                            store_row(2, rd_mem)
                            pool.wait_ge(made_done, 3 * NB)
                        fetch(b - 1)
                    if c == STORE_OUT:
                        store_out(b - 1)

            last(1, 1)
            with pool.Fori(1, NB // 2 - 1) as pair:
                for half in range(2):
                    last(2 * pair + half, half)
            last(NB - 2, 0)
            last(NB - 1, 1)
            fetch(NB - 1)

        @block.scalar
        def _(act):
            def split_w(n):
                act.wait_ge(w_loaded[n], 16)
                if n == 3:
                    act.wait_ge(made_done, NB)
                nc.scalar.activation(w_hi[:, W_ORDER[n][1], :, :], w_raw[n], ACT.Copy).then_inc(w_hi_ready, 1)

            def ln_root(n, width):
                act.wait_ge(var_ready, n)
                nc.scalar.activation(root[:, 0:width], var[:, 0:width], ACT.Sqrt).then_inc(root_ready, 1)

            def g_hi_from(source, dest, b):
                nc.scalar.activation(dest[:, tiles(b), :], source, ACT.Copy).then_inc(g_hi_ready, 1)

            def head_norm(b):
                act.wait_ge(rstd_ready, b // 2 + 1)
                for t in range(IT):
                    n = b % 2 * IT + t
                    ins = nc.scalar.activation(x_all[:, b, t, :], x_all[:, b, t, :], ACT.Relu,
                                               bias=shift[:, n:n + 1], scale=rstd[:, n:n + 1])
                ins.then_inc(normed, 1)

            def head_h(b):
                act.wait_ge(turned_done, b + 1)
                if b >= HEAD_RING:
                    act.wait_ge(head_stored[b % HEAD_RING], 32 * (b // HEAD_RING))
                    act.wait_ge(made_done, b - HEAD_RING + 1)
                nc.scalar.activation(head_part(HI, b).rearrange("p (k n) -> p k n", k=K), turned[:, :, :],
                                     ACT.Copy).then_inc(h_hi_ready, 1)

            def head_g(b):
                act.wait_ge(made_done, b + 1)
                g_hi_from(made_of[b % 2], g_hi[0], b)

            def after_graph_1(c, q, b, half):
                if c == TAKE:
                    act.wait_ge(chunk_done, q * NC)
                    if not is_at(q, 1):
                        act.wait_ge(h_stored, (q - 1) * 16)
                        act.wait_ge(made_done, q + (NB - 1))
                    nc.scalar.activation(h_new[:, HI, :, :], main[:, half, :, :], ACT.Relu).then_inc(h_hi_ready, 1)
                if c == SPLIT_MADE_HI:
                    act.wait_ge(made_done, q + NB)
                    g_hi_from(made[:, :, :], g_hi[1], b)

            def after_graph_2(c, q, b, half):
                late = is_at(q, 2 * NB)
                if c == (ROOT_HYPER if late else ROOT):
                    ln_root(q - NB + LN_HEAD, IT)
                if c == (NORM_HYPER if late else NORM):
                    act.wait_ge(rstd_ready, q - NB + LN_HEAD)
                    if is_at(q, NB + 1):
                        act.wait_ge(cols_done, NB)
                    else:
                        act.wait_ge(g_lo_ready, q + (NB - 1))
                        act.wait_ge(g_stored, (q - (NB + 1)) * 16)
                    for t in range(IT):
                        ins = nc.scalar.activation(nat[:, t, :], made[:, t, :], ACT.Relu,
                                                   bias=shift[:, t:t + 1], scale=rstd[:, t:t + 1])
                    ins.then_inc(normed, 1)
                    act.wait_ge(normed, q)
                    g_hi_from(nat[:, :, :], g_hi[0], b)

            def after_counts(c, q, dest, b):
                if c == COUNT_TAKE:
                    act.wait_ge(cols_done, q)
                    nc.scalar.activation(dest[:, tiles(b)], turned[:, 0, 0:2 * IT:2], ACT.Copy).then_inc(cols_taken, 1)

            def take_row(number):
                act.wait_ge(row_turned, number)
                if number > 1:
                    act.wait_ge(pre_stored, 16 * (NB - PRE_FROM) * len(PRE) + 16)
                nc.scalar.activation(row, turned[0:N // P, 0, 0:P], ACT.Copy).then_inc(row_ready, 1)

            def split_chunk(q, layer, c):
                if layer == HYPER:
                    wait_inc(act, q, c)
                else:
                    wait_raw(act, q, layer, c)
                if not (is_first(q) and c < HI_RING):
                    act.wait_ge(chunk_done, last_of_slot(q, layer, c, HI_RING))
                nc.scalar.activation(hi[:, slot(q, layer, c, HI_RING), :], raw_at(layer, c), ACT.Copy
                                     ).then_inc(hi_ready, 1)

            act.wait_ge(const_step, 2)
            nc.scalar.activation(col_b[:, 0:2], ones[:, :], ACT.Sqrt)
            nc.scalar.activation(ones_r[:, :], ones[:, :], ACT.Copy).then_inc(ones_ready, 1)
            ln_root(1, 2 * IT)
            head_norm(0)
            split_w(0)
            for b in range(NB):
                head_h(b)
                if b + 1 < NB:
                    head_norm(b + 1)
                for c in head_chunks(b - 1):
                    split_chunk(0, GRAPH_1, c)
                if b % 2 == 0 and b + 2 < NB:
                    ln_root(b // 2 + 2, 2 * IT)
                if b < 2:
                    split_w(b + 1)
                head_g(b)
            split_w(3)
            for c in head_chunks(NB - 1):
                split_chunk(0, GRAPH_1, c)

            def one(q, layer, b, half):
                for c in range(NC):
                    if not whole(q, layer, c):
                        split_chunk(q, layer, c)
                    if not is_first(q):
                        was, last_b = before(q, layer, b)
                        if was == GRAPH_1:
                            after_graph_1(c, q, last_b, 1 - half)
                            after_counts(c, q, cnt, last_b)
                        if was == GRAPH_2:
                            after_graph_2(c, q, last_b, 1 - half)
                            after_counts(c, q, rsum, last_b)
                    if is_at(q, NB) and c == NC - 1:
                        act.wait_ge(cols_step, 1)
                        nc.scalar.activation(col_b[:, :], col_a[:, :], ACT.Sqrt).then_inc(norm_root, 1)
                    if is_at(q, NB + 1) and c == 5:
                        take_row(1)
                    if is_at(q, 2 * NB + 1) and c == 3:
                        take_row(2)

            blocks(act, one)

        @block.vector
        def _(dve):
            def lo_of(dest, value, high, relu=False):
                if relu:
                    return nc.vector.scalar_tensor_tensor(out=dest, in0=value, scalar=0.0, in1=high.bitcast(f32),
                                                          op0=ALU.max, op1=ALU.subtract)
                return nc.vector.tensor_tensor(dest, value, high.bitcast(f32), ALU.subtract)

            def split_w(n):
                dve.wait_ge(w_hi_ready, n + 1)
                lo_of(w_lo[:, W_ORDER[n][1], :, :], w_raw[n], w_hi[:, W_ORDER[n][1], :, :]).then_inc(w_lo_ready, 1)

            def ln_sums(sources, at=0):
                for t, source in enumerate(sources):
                    ins = nc.vector.bn_stats(stats[:, at + t, :], source)
                return ins

            def ln_stats(sums, n, width):
                step = (n - 1) * LN_STEPS
                sums.then_inc(ln_step, 1)
                dve.wait_ge(ln_step, step + 1)
                dve.sem_inc(stats_seen, 1)
                for t in range(width):
                    ins = nc.vector.bn_aggr(mv[:, t, :], stats[:, t, :])
                ins.then_inc(ln_step, 1)
                dve.wait_ge(ln_step, step + 2)
                nc.vector.tensor_scalar(var[:, 0:width], mv[:, 0:width, 1], LN_EPS, None, ALU.add
                                        ).then_inc(var_ready, 1)
                nc.vector.tensor_scalar(nmean2[:, 0:width], mv[:, 0:width, 0], -2.0, None, ALU.mult
                                        ).then_inc(ln_step, 1)

            def ln_rstd(n, width):
                step = (n - 1) * LN_STEPS
                part = slice(0, width)
                dve.wait_ge(root_ready, n)
                nc.vector.reciprocal(quot[:, part], root[:, part]).then_inc(ln_step, 1)
                dve.wait_ge(ln_step, step + 4)
                nc.vector.tensor_tensor(quot[:, part], quot[:, part], var[:, part], ALU.mult).then_inc(ln_step, 1)
                dve.wait_ge(ln_step, step + 5)
                nc.vector.tensor_tensor(quot[:, part], quot[:, part], root[:, part], ALU.add).then_inc(ln_step, 1)
                dve.wait_ge(ln_step, step + 6)
                nc.vector.reciprocal(quot[:, part], quot[:, part]).then_inc(quot_ready, 1)
                dve.wait_ge(quot_ready, n)
                nc.vector.tensor_scalar(rstd[:, part], quot[:, part], 2.0, None, ALU.mult)
                nc.vector.tensor_tensor(shift[:, part], quot[:, part], nmean2[:, part], ALU.mult
                                        ).then_inc(rstd_ready, 1)

            def head_sums(b):
                return ln_sums([x_all[:, b, t, :] for t in range(IT)], b % 2 * IT)

            def head_h(b):
                dve.wait_ge(h_hi_ready, b + 1)
                lo_of(head_part(LO, b).rearrange("p (k n) -> p k n", k=K), turned[:, :, :],
                      head_part(HI, b).rearrange("p (k n) -> p k n", k=K)).then_inc(h_lo_ready, 1)

            def head_g(b):
                dve.wait_ge(g_hi_ready, b + 1)
                lo_of(g_lo[0][:, tiles(b), :], made_of[b % 2], g_hi[0][:, tiles(b), :]).then_inc(g_lo_ready, 1)

            def sum_chunk(q, layer, c):
                chunk = raw_at(layer, c)
                if not (is_first(q) and c == 0):
                    dve.wait_ge(acc_step, q * NC + c)
                dest = acc[:, :]
                if c == NC - 1 and layer == GRAPH_1:
                    dest = acc_end[layer]
                    if not is_first(q):
                        dve.wait_ge(cols_done, q)
                if c == 0 and layer == GRAPH_2 and not is_at(q, NB):
                    dve.wait_ge(fold_ready, q)
                if layer == GRAPH_1 and c == 0:
                    ins = nc.vector.tensor_scalar(dest, chunk, 0.0, None, ALU.is_gt)
                elif layer == GRAPH_1:
                    ins = nc.vector.scalar_tensor_tensor(out=dest, in0=chunk, scalar=0.0, in1=acc[:, :],
                                                         op0=ALU.is_gt, op1=ALU.add)
                elif c == 0:
                    ins = nc.vector.tensor_copy(dest, chunk)
                else:
                    ins = nc.vector.tensor_tensor(dest, acc[:, :], chunk, ALU.add)
                ins.then_inc(acc_step, 1)

            def fold(number, was):
                dve.wait_ge(acc_step, number * NC)
                if was == GRAPH_2:
                    dve.wait_ge(cols_done, number - 1)
                if is_at(number, NB + 1):
                    dve.wait_ge(h_stored, 16 * NB)
                nc.vector.tensor_tensor(folded[was], acc_end[was][:, 0:BW], acc_end[was][:, BW:CW],
                                        ALU.add).then_inc(fold_ready, 1)

            def make_pre(q, b, half, c):
                number = pre_number(b, c)
                dve.wait_ge(rn_loaded[half], (b - half) * 8)
                dve.wait_ge(pre_stored, number * 16 + 16)
                scale = rn_row[:, half, :].rearrange("p (a n) -> p a n", a=1).broadcast_to([P, CT, BW])
                nc.vector.scalar_tensor_tensor(
                    out=pre[:, :].rearrange("p (t n) -> p t n", t=CT),
                    in0=raw_at(GRAPH_2, c).rearrange("p (t n) -> p t n", t=CT), scalar=0.0, in1=scale,
                    op0=ALU.is_gt, op1=ALU.mult).then_inc(pre_step, 1)
                split_chunk(q, GRAPH_2, c)
                dve.wait_ge(pre_step, number + 1)
                nc.vector.tensor_tensor(pre[:, :], raw_at(GRAPH_2, c), pre[:, :], ALU.add).then_inc(pre_ready, 1)

            def split_chunk(q, layer, c):
                if not (is_first(q) and c < LO_RING):
                    dve.wait_ge(chunk_done, lo_free(q, layer, c))
                dve.wait_ge(hi_ready, splits(q, layer, c + 1))
                lo_of(lo_at(q, layer, c), raw_at(layer, c),
                      hi[:, slot(q, layer, c, HI_RING), :]).then_inc(lo_ready, 1)

            def step_at(q, c):
                if by_dma(q, c):
                    return step_added[:, add_slot(c), :]
                if is_at(q, 2 * NB):
                    return acc[:, :] if c % 2 == 0 or c < RING else step_more[:, :]
                turn = sum(not by_dma(q, a) and not made_before(q, a) for a in range(c))
                return acc[:, :] if turn % 2 == 0 else step_more[:, :]

            def incidence(q, c, half):
                scale = rn_row[:, half, :].rearrange("p (a n) -> p a n", a=1).broadcast_to([P, CT, BW])
                if is_at(q, 2 * NB) and c == 0:
                    dve.wait_ge(fold_ready, q)
                elif is_at(q, 2 * NB) and c == RING + 1:
                    dve.wait_ge(chunk_done, q * NC)
                elif is_at(q, 2 * NB) and c <= RING:
                    dve.wait_ge(inc_ready, sums(q, c))
                elif not by_dma(q, c):
                    dve.wait_ge(inc_ready, sums(q, c) - 1)
                elif is_at(q, 2 * NB + 1) and ADDED.index(c) < ADD_RING:
                    dve.wait_ge(h_used, 2 * NB * K)
                else:
                    dve.wait_ge(inc_added[add_slot(c)], added(q, c) - 16)
                nc.vector.scalar_tensor_tensor(
                    out=step_at(q, c).rearrange("p (t n) -> p t n", t=CT),
                    in0=raw_at(HYPER, c).rearrange("p (t n) -> p t n", t=CT), scalar=0.0, in1=scale,
                    op0=ALU.is_gt, op1=ALU.mult).then_inc(acc_step, 1)

            def add_incidence(q, c):
                dve.wait_ge(acc_step, steps(q, c + 1))
                nc.vector.tensor_tensor(raw_at(HYPER, c), raw_at(HYPER, c), step_at(q, c),
                                        ALU.add).then_inc(inc_ready, 1)

            def behind(q, layer, c):
                early = is_at(q, 2 * NB)
                old_q, _, old_c = chunk_before(q, layer, c, 1)
                if not (early and c <= RING) and not by_dma(old_q, old_c) and not made_before(old_q, old_c):
                    add_incidence(old_q, old_c)
                lag = 1 if early and c <= RING else 2
                old_q, old_layer, old_c = chunk_before(q, layer, c, lag)
                if early and c == RING + 1:
                    return
                if old_layer == HYPER and not whole(old_q, old_layer, old_c):
                    split_chunk(old_q, old_layer, old_c)

            def after_graph_1(c, q, b, half):
                if c == TAKE:
                    dve.wait_ge(h_hi_ready, q + NB)
                    lo_of(h_new[:, LO, :, :], main[:, half, :, :], h_new[:, HI, :, :],
                          relu=True).then_inc(h_lo_ready, 1)
                if c == SPLIT_MADE:
                    if is_at(q, 1):
                        for ring in head_stored:
                            dve.wait_ge(ring, 32 * NB // HEAD_RING)
                    dve.wait_ge(g_hi_ready, q + NB)
                    lo_of(g_lo[1][:, tiles(b), :], made[:, :, :], g_hi[1][:, tiles(b), :]).then_inc(g_lo_ready, 1)

            def after_graph_2(c, q, b, half):
                if c == (TAKE_HYPER if is_at(q, 2 * NB) else TAKE):
                    dve.wait_ge(chunk_done, q * NC)
                    dve.wait_ge(xblk_loaded, (q - NB) * 16)
                    nc.vector.scalar_tensor_tensor(out=xblk[:, :, :], in0=main[:, half, :, :], scalar=0.0,
                                                   in1=xblk[:, :, :], op0=ALU.max, op1=ALU.add
                                                   ).then_inc(xblk_ready, 1)
                late = is_at(q, 2 * NB)
                if c == (STATS_HYPER if late else STATS):
                    dve.wait_ge(made_done, q + NB)
                    ln_stats(ln_sums([made[:, t, :] for t in range(IT)]), q - NB + LN_HEAD, IT)
                if c == (RSTD_HYPER if late else RSTD):
                    ln_rstd(q - NB + LN_HEAD, IT)
                if c == (SPLIT_NORM_HYPER if late else SPLIT_NORM):
                    dve.wait_ge(g_hi_ready, q + NB)
                    lo_of(g_lo[0][:, tiles(b), :], nat[:, :, :], g_hi[0][:, tiles(b), :]).then_inc(g_lo_ready, 1)

            def after_hyper(q, half):
                dve.wait_ge(chunk_done, q * NC)
                dve.wait_ge(rd_loaded, (q - 2 * NB) * 16)
                scale = rd_row[:, 0:BW].rearrange("p (a n) -> p a n", a=1).broadcast_to([P, K, BW])
                result = nat[:, :, :].rearrange("p t d -> p (t d)").rearrange("p (k n) -> p k n", k=K)
                nc.vector.tensor_tensor(result, main[:, half, :, :], scale, ALU.mult).then_inc(product, 1)
                dve.wait_ge(product, q - 2 * NB)
                dve.wait_ge(xblk_loaded, (q - NB) * 16)
                nc.vector.tensor_tensor(xblk[:, :, :], result, xblk[:, :, :], ALU.add).then_inc(xblk_ready, 1)

            def norms():
                dve.wait_ge(norm_root, 1)
                nc.vector.reciprocal(rn[:, :], col_b[:, :]).then_inc(cols_step, 1)
                dve.wait_ge(cols_step, 2)
                nc.vector.tensor_tensor(rn[:, :], rn[:, :], col_a[:, :], ALU.mult).then_inc(cols_step, 1)
                dve.wait_ge(cols_step, 3)
                nc.vector.tensor_tensor(rn[:, :], rn[:, :], col_b[:, :], ALU.add).then_inc(cols_step, 1)
                dve.wait_ge(cols_step, 4)
                nc.vector.tensor_scalar(rn[:, :], rn[:, :], 0.5, NORM_EPS, ALU.mult, ALU.max).then_inc(cols_step, 1)
                dve.wait_ge(cols_step, 5)
                nc.vector.reciprocal(rn[:, :], rn[:, :]).then_inc(cols_step, 1)

            def degrees():
                dve.wait_ge(cols_taken, 2 * NB)
                nc.vector.tensor_tensor(col_a[:, :], cnt[:, :], rn[:, :], ALU.mult).then_inc(cols_step, 1)
                dve.wait_ge(cols_step, 7)
                nc.vector.tensor_tensor(col_a[:, :], col_a[:, :], rsum[:, :], ALU.add).then_inc(cols_step, 1)
                dve.wait_ge(cols_step, 8)
                nc.vector.reciprocal(rdeg[:, :], col_a[:, :]).then_inc(cols_step, 1)

            def head_chunk(c):
                wait_raw(dve, 0, GRAPH_1, c)
                sum_chunk(0, GRAPH_1, c)
                split_chunk(0, GRAPH_1, c)

            dve.wait_ge(x_first, 16)
            head_sums(0)
            dve.wait_ge(x_loaded[0], 16)
            ln_stats(head_sums(1), 1, 2 * IT)
            ln_rstd(1, 2 * IT)
            split_w(0)
            for b in range(NB):
                chunks = head_chunks(b - 1)
                stats_now = b % 2 == 0 and b + 2 < NB
                head_h(b)
                for c in chunks[:1]:
                    head_chunk(c)
                if stats_now:
                    dve.wait_ge(x_loaded[b // 2 + 1], 16)
                    dve.wait_ge(normed, b + 2)
                    head_sums(b + 2)
                    ln_stats(head_sums(b + 3), b // 2 + 2, 2 * IT)
                for c in chunks[1:]:
                    head_chunk(c)
                if stats_now:
                    ln_rstd(b // 2 + 2, 2 * IT)
                if b < 2:
                    split_w(b + 1)
                head_g(b)
            split_w(3)
            for c in head_chunks(NB - 1):
                head_chunk(c)

            def one(q, layer, b, half):
                for c in range(NC):
                    wait_raw(dve, q, layer, c)
                    if layer == HYPER:
                        if c == 0:
                            dve.wait_ge(rn_loaded[half], (b - half) * 8 + 16 * (NB // 2))
                        if is_at(q, 2 * NB) and 0 < c <= RING:
                            add_incidence(q, c - 1)
                        if not made_before(q, c):
                            incidence(q, c, half)
                        behind(q, layer, c)
                    else:
                        sum_chunk(q, layer, c)
                        if layer == GRAPH_2 and made_before(q + NB, c):
                            make_pre(q, b, half, c)
                        else:
                            split_chunk(q, layer, c)
                    if not is_first(q):
                        was, last_b = before(q, layer, b)
                        if was == GRAPH_1:
                            after_graph_1(c, q, last_b, 1 - half)
                        if was == GRAPH_2:
                            after_graph_2(c, q, last_b, 1 - half)
                        if was == GRAPH_1 and c == FOLD:
                            fold(q, was)
                        if was == HYPER and c == FINISH:
                            after_hyper(q, 1 - half)
                    if is_at(q, NB) and c == NC - 2:
                        dve.wait_ge(cols_taken, NB)
                        nc.vector.tensor_scalar(col_a[:, :], cnt[:, :], NORM_EPS * NORM_EPS, None,
                                                ALU.max).then_inc(cols_step, 1)
                    if is_at(q, NB) and c == NC - 1:
                        norms()
                    if layer == GRAPH_2 and c == NC - 1:
                        fold(q + 1, GRAPH_2)
                    if is_at(q, 2 * NB) and c == NC - 1:
                        degrees()

            blocks(dve, one)
            behind(3 * NB, HYPER, 0)
            split_chunk(3 * NB - 1, HYPER, NC - 1)
            dve.wait_ge(rd_loaded, NB * 16)
            dve.wait_ge(xblk_loaded, 2 * NB * 16)
            for k in range(K):
                dve.wait_ge(*((group_done, NB), (chunk_done, 3 * NB * NC))[k])
                result = nat[:, 2 * k:2 * k + 2, :].rearrange("p t d -> p (t d)")
                nc.vector.tensor_tensor(result, main[:, 1, k, :], rd_row[:, 0:BW], ALU.mult).then_inc(product, 1)
                dve.wait_ge(product, NB + k)
                nc.vector.tensor_tensor(xblk[:, k, :], result, xblk[:, k, :], ALU.add).then_inc(xblk_ready, 1)

        @block.tensor
        def _(pe):
            def three(dest, stationary, moving, start, stop):
                nc.tensor.matmul(dest, stationary[HI], moving[HI], start=start, stop=False)
                nc.tensor.matmul(dest, stationary[LO], moving[HI], start=False, stop=False)
                return nc.tensor.matmul(dest, stationary[HI], moving[LO], start=False, stop=stop)

            def times_wb(dest, h):
                for t in range(IT):
                    for k in range(K):
                        ins = three(dest[:, t, :], [part[:, k, t * P:(t + 1) * P] for part in h],
                                    (w_hi[:, WB, k, :], w_lo[:, WB, k, :]), k == 0, k == K - 1)
                ins.then_inc(made_done, 1)

            def head_turn(b):
                pe.wait_ge(normed, b + 1)
                if b:
                    pe.wait_ge(h_lo_ready, b)
                for t in range(IT):
                    for k in range(K):
                        ins = nc.tensor.transpose(turned[:, k, t * P:(t + 1) * P],
                                                  x_all[:, b, t, k * P:(k + 1) * P], ident[:, :])
                ins.then_inc(turned_done, 1)

            def head_times(b):
                pe.wait_ge(h_lo_ready, b + 1)
                if b >= 2:
                    pe.wait_ge(g_lo_ready, b - 1)
                times_wb(made_of[b % 2], [head_part(part, b).rearrange("p (k n) -> p k n", k=K)
                                          for part in (HI, LO)])

            def times_wa(q, layer, half, k):
                pe.wait_ge(h_loaded, q * (16 * K) + 16 * (k + 1))
                place = (WA_1, WA_2)[layer]
                for f in range(K):
                    weight = [m[:, place, k, f * P:(f + 1) * P] for m in (w_hi, w_lo)]
                    ins = three(main[:, half, f, :], weight, [h_old[:, s, :] for s in (HI, LO)], False, False)
                ins.then_inc(h_used, 1)

            def made_free(number):
                pe.wait_ge(g_hi_ready, number - 1)
                pe.wait_ge(g_lo_ready, number - 1)

            def sum_columns(q, was):
                pe.wait_ge(fold_ready, q)
                if not is_at(q, 1):
                    pe.wait_ge(cols_taken, q - 1)
                if is_at(q, NB + 1):
                    pe.wait_ge(row_ready, 1)
                for t in range(IT):
                    ins = nc.tensor.matmul(turned[:, 0, 2 * t:2 * t + 2], folded[was][:, t * P:(t + 1) * P],
                                           (ones_r, ones)[was][:, :], start=True, stop=True)
                ins.then_inc(cols_done, 1)

            def turn_cols(source, step, number):
                pe.wait_ge(cols_step, step)
                pe.wait_ge(cols_taken, number * NB)
                nc.tensor.transpose(turned[0:N // P, 0, 0:P], source[:, :], ident[:, :]).then_inc(row_turned, 1)

            def after_graph_1(c, q):
                if c == MAKE:
                    if is_at(q, 1):
                        pe.wait_ge(w_lo_ready, 4)
                    pe.wait_ge(h_lo_ready, q + NB)
                    made_free(q + NB)
                    times_wb(made, [h_new[:, s, :, :] for s in (HI, LO)])

            def after_graph_2(c, q):
                if c == MAKE:
                    pe.wait_ge(xblk_ready, q - NB)
                    made_free(q + NB)
                    for t in range(IT):
                        for k in range(K):
                            ins = nc.tensor.transpose(made[:, t, k * P:(k + 1) * P],
                                                      xblk[:, k, t * P:(t + 1) * P], ident[:, :])
                    ins.then_inc(made_done, 1)

            def products(q, layer, b, half, c):
                ends = c == NC - 1
                if whole(q, layer, c):
                    if is_at(q, 2 * NB) or is_at(q, 2 * NB + 1):
                        pe.wait_ge(g_loaded[c * CT // IT], 16)
                    wait_inc(pe, q, c)
                    for s in range(CT):
                        for f in range(K):
                            ins = nc.tensor.matmul(main[:, half, f, :],
                                                   g_whole[:, c * CT + s, f * P:(f + 1) * P],
                                                   raw_at(layer, c)[:, s * BW:(s + 1) * BW],
                                                   start=c + s == 0, stop=ends and s == CT - 1)
                else:
                    pe.wait_ge(hi_ready, splits(q, layer, c + 1))
                    pe.wait_ge(lo_ready, splits(q, layer, c + 1))
                    parts = (hi[:, slot(q, layer, c, HI_RING), :], lo_at(q, layer, c))
                    for f in range(K):
                        for s in range(CT):
                            g = [m[layer % 2][:, c * CT + s, f * P:(f + 1) * P] for m in (g_hi, g_lo)]
                            ins = three(main[:, half, f, :], g, [part[:, s * BW:(s + 1) * BW] for part in parts],
                                        c + s == 0, ends and s == CT - 1)
                        if layer == HYPER and ends and f == 0:
                            ins.then_inc(group_done, 1)
                ins.then_inc(chunk_done, 1)
                if layer != HYPER and c in WA_AT:
                    times_wa(q, layer, half, WA_AT.index(c))

            def head_products(b):
                for c in head_chunks(b):
                    pe.wait_ge(g_lo_ready, b + 1)
                    if c == WA_AT[0]:
                        pe.wait_ge(w_lo_ready, 2)
                    products(0, GRAPH_1, 0, 0, c)

            pe.wait_ge(const_step, 3)
            for b in range(NB):
                head_turn(b)
                head_products(b - 2)
                if b == 0:
                    pe.wait_ge(w_lo_ready, 1)
                head_times(b)
            head_products(NB - 2)
            head_products(NB - 1)
            pe.wait_ge(w_lo_ready, 3)
            pe.wait_ge(ones_ready, 1)

            def one(q, layer, b, half):
                if not is_at(q, 1):
                    if layer == GRAPH_1 or is_at(q, NB) or is_at(q, NB + 1):
                        pe.wait_ge(h_lo_ready, q + (NB - 1))
                    else:
                        pe.wait_ge(xblk_ready, q - (NB + 1))
                if isinstance(b, int) and b == 0:
                    pe.wait_ge(g_lo_ready, (layer + 1) * NB - 1)
                for c in range(NC):
                    if isinstance(b, int) and b == 0 and c * CT == (NB - 1) * IT:
                        pe.wait_ge(g_lo_ready, (layer + 1) * NB)
                    products(q, layer, b, half, c)
                    was, last_b = before(q, layer, b)
                    if was == GRAPH_1:
                        after_graph_1(c, q)
                    if was == GRAPH_2:
                        after_graph_2(c, q)
                    if was != HYPER and c == COUNT:
                        sum_columns(q, was)
                    if is_at(q, NB + 1) and c == 1:
                        turn_cols(rn, 6, 1)
                    if is_at(q, 2 * NB + 1) and c == 1:
                        turn_cols(rdeg, 9, 2)

            blocks(pe, one)


def kernel(x, adj, L0_gnn_W1, L0_gnn_W2):
    import numpy as np
    import concourse.bacc as bacc
    from concourse.bass_utils import run_bass_kernel_spmd

    x, adj, w1, w2 = (np.asarray(a) for a in (x, adj, L0_gnn_W1, L0_gnn_W2))
    f32 = mybir.dt.float32
    arrays = {
        "adj_t": adj.reshape(NB, BW, NC, CT, P).transpose(0, 2, 4, 3, 1).reshape(NB, NC, P, CW),
        "x_rows": x.reshape(NB, IT, P, D).transpose(0, 2, 1, 3),
        "x_cols": x.reshape(NB, BW, K, P).transpose(0, 3, 2, 1).reshape(NB, P, K * BW),
        "w": np.stack([w1, w2]).reshape(4, K, P, D).transpose(0, 2, 1, 3),
    }
    arrays = {name: np.ascontiguousarray(a) for name, a in arrays.items()}
    nc = bacc.Bacc("TRN2", target_bir_lowering=False, num_devices=1)
    ins = [nc.dram_tensor(name, a.shape, f32, kind="ExternalInput").ap() for name, a in arrays.items()]
    out = nc.dram_tensor("out", (NB, P, K * BW), f32, kind="ExternalOutput").ap()
    h_mem = nc.dram_tensor("h_mem", (2, NB, K, P, 2, BW), f32, kind="Internal").ap()
    g_mem = nc.dram_tensor("g_mem", (NB, P, IT, D), f32, kind="Internal").ap()
    x1_mem = nc.dram_tensor("x1_mem", (NB, P, K * BW), f32, kind="Internal").ap()
    rn_mem = nc.dram_tensor("rn_mem", (NB, BW), f32, kind="Internal").ap()
    rd_mem = nc.dram_tensor("rd_mem", (NB, BW), f32, kind="Internal").ap()
    inc_mem = nc.dram_tensor("inc_mem", (NB, len(PRE), P, CW), f32, kind="Internal").ap()
    gnn_kernel(nc, *ins, out, h_mem, g_mem, x1_mem, rn_mem, rd_mem, inc_mem)
    result = run_bass_kernel_spmd(nc, [arrays], core_ids=[0]).results[0]["out"]
    return np.ascontiguousarray(result.reshape(NB, P, K, BW).transpose(0, 3, 2, 1)).reshape(N, D)
```
